# Optimizing a Trainium2 kernel written in Bass

```python
import numpy as np
import jax
import jax.numpy as jnp

def _softmax(x, axis=-1):
    return jax.nn.softmax(x, axis=axis)

def _gelu(x):
    return jax.nn.gelu(x, approximate=True)

def _silu(x):
    return jax.nn.silu(x)

def _sigmoid(x):
    return jax.nn.sigmoid(x)

def _layernorm(x, axis=-1, eps=1e-05):
    m = jnp.mean(x, axis=axis, keepdims=True)
    v = jnp.var(x, axis=axis, keepdims=True)
    return (x - m) / jnp.sqrt(v + eps)

def _scatter_add(tgt, idx, src, axis=0):
    return tgt.at[idx].add(src)

def _segment_sum(src, seg, n):
    return jax.ops.segment_sum(src, seg, n)
kernel_name = 'mk_seq_postln_d1_jaxref_r4_719219'

def setup_inputs(seed: int=0):
    np.random.seed(seed)
    _w = jnp.asarray

    def _L0_attn_setup():
        import jax, jax.numpy as jnp
        import numpy as np
        D_MODEL, D_STATE, DT_RANK = (256, 16, 64)
        B_SZ, T_LEN = (2, 512)
        key = jax.random.key(seed)
        k1, k2, k3, k4 = jax.random.split(key, 4)
        x = jax.random.normal(k1, (B_SZ, T_LEN, D_MODEL), dtype=jnp.float32)
        W_xproj = jax.random.normal(k2, (DT_RANK + 2 * D_STATE, D_MODEL), dtype=jnp.float32) / np.sqrt(D_MODEL)
        W_dt = 0.01 * jax.random.normal(k3, (D_MODEL, DT_RANK), dtype=jnp.float32)
        b_dt = jax.random.uniform(k4, (D_MODEL,), dtype=jnp.float32, minval=-np.log(D_STATE), maxval=np.log(D_STATE))
        A_log = jnp.log(jnp.arange(1, D_STATE + 1, dtype=jnp.float32))[None, :].repeat(D_MODEL, axis=0)
        Dp = jnp.ones((D_MODEL,), dtype=jnp.float32)
        return {'x': x, 'W_xproj': W_xproj, 'W_dt': W_dt, 'b_dt': b_dt, 'A_log': A_log, 'Dp': Dp}
    _L0_attn_in = _L0_attn_setup()

    def _L0_ffn_setup():
        import jax, jax.numpy as jnp
        import numpy as np
        DIM = 256
        HIDDEN = 768
        SCALE = 1.0 / 127.0

        def _dequant(w_int, dtype):
            return w_int.astype(dtype) * jnp.asarray(SCALE, dtype)
        key = jax.random.key(seed)
        k_x, k_g, k_u, k_d = jax.random.split(key, 4)
        x = jax.random.normal(k_x, (4, 512, DIM), dtype=jnp.float32)
        w_gate = jax.random.randint(k_g, (HIDDEN, DIM), -127, 128, dtype=jnp.int32)
        w_up = jax.random.randint(k_u, (HIDDEN, DIM), -127, 128, dtype=jnp.int32)
        w_down = jax.random.randint(k_d, (DIM, HIDDEN), -127, 128, dtype=jnp.int32)
        return {'x': x, 'w_gate': w_gate, 'w_up': w_up, 'w_down': w_down}
    _L0_ffn_in = _L0_ffn_setup()
    _d = {'L0_attn_x': _L0_attn_in['x'], 'L0_attn_W_xproj': _L0_attn_in['W_xproj'], 'L0_attn_W_dt': _L0_attn_in['W_dt'], 'L0_attn_b_dt': _L0_attn_in['b_dt'], 'L0_attn_A_log': _L0_attn_in['A_log'], 'L0_attn_Dp': _L0_attn_in['Dp'], 'L0_ffn_w_gate': _L0_ffn_in['w_gate'], 'L0_ffn_w_up': _L0_ffn_in['w_up'], 'L0_ffn_w_down': _L0_ffn_in['w_down']}
    _x0 = _d['L0_attn_x']
    _d['L0_attn_x'] = jax.random.normal(jax.random.fold_in(jax.random.key(seed), 1), (16, 1024, 256), dtype=_x0.dtype)
    del _x0
    return _d

def reference(L0_attn_x, L0_attn_W_xproj, L0_attn_W_dt, L0_attn_b_dt, L0_attn_A_log, L0_attn_Dp, L0_ffn_w_gate, L0_ffn_w_up, L0_ffn_w_down):

    def _L0_attn_ref(x, W_xproj, W_dt, b_dt, A_log, Dp):
        import jax, jax.numpy as jnp
        import numpy as np
        D_MODEL, D_STATE, DT_RANK = (256, 16, 64)
        B_SZ, T_LEN = (2, 512)
        dt_rank = W_dt.shape[1]
        d_s = A_log.shape[1]
        xz = jnp.einsum('btd,pd->btp', x, W_xproj)
        dt_raw = xz[..., :dt_rank]
        Bm = xz[..., dt_rank:dt_rank + d_s]
        Cm = xz[..., dt_rank + d_s:]
        dt = jax.nn.softplus(jnp.einsum('btr,dr->btd', dt_raw, W_dt) + b_dt)
        A = -jnp.exp(A_log)
        dA = jnp.exp(dt[..., None] * A)
        dBx = dt[..., None] * Bm[:, :, None, :] * x[..., None]

        def step(h, inp):
            dA_t, dBx_t, C_t = inp
            h = dA_t * h + dBx_t
            y = jnp.einsum('bds,bs->bd', h, C_t)
            return (h, y)
        h0 = jnp.zeros((x.shape[0], x.shape[2], d_s), dtype=x.dtype)
        _, ys = jax.lax.scan(step, h0, (dA.transpose(1, 0, 2, 3), dBx.transpose(1, 0, 2, 3), Cm.transpose(1, 0, 2)))
        out = ys.transpose(1, 0, 2)
        return out + Dp * x

    def _L0_ffn_ref(x, w_gate, w_up, w_down):
        import jax, jax.numpy as jnp
        import numpy as np
        DIM = 256
        HIDDEN = 768
        SCALE = 1.0 / 127.0

        def _dequant(w_int, dtype):
            return w_int.astype(dtype) * jnp.asarray(SCALE, dtype)
        wg = _dequant(w_gate, x.dtype)
        wu = _dequant(w_up, x.dtype)
        wd = _dequant(w_down, x.dtype)
        gate = jnp.einsum('bsd,hd->bsh', x, wg)
        up = jnp.einsum('bsd,hd->bsh', x, wu)
        h = jax.nn.silu(gate) * up
        return jnp.einsum('bsh,dh->bsd', h, wd)
    x = L0_attn_x
    x = _layernorm(x + _L0_attn_ref(x, L0_attn_W_xproj, L0_attn_W_dt, L0_attn_b_dt, L0_attn_A_log, L0_attn_Dp), axis=-1)
    x = _layernorm(x + _L0_ffn_ref(x, L0_ffn_w_gate, L0_ffn_w_up, L0_ffn_w_down), axis=-1)
    return x

_drawn_inputs = setup_inputs


def setup_inputs(seed=0):
    import zlib

    import numpy as np

    out = dict(_drawn_inputs(seed))
    spreads = {'L0_attn_Dp': (1.0, 0.2)}
    factors = {}
    for name, (base, spread) in spreads.items():
        noise = np.random.default_rng([zlib.crc32(name.encode()), seed]).standard_normal(out[name].shape)
        drawn = base * np.exp(spread * noise) if base else spread * noise
        out[name] = jnp.asarray(drawn.astype(out[name].dtype))
    for name, factor in factors.items():
        out[name] = (out[name] * factor).astype(out[name].dtype)
    return out
```

```python
from contextlib import ExitStack

import concourse.bass as bass
from concourse import mybir

P = 128
F32 = mybir.dt.float32
BF16 = mybir.dt.bfloat16
F16 = mybir.dt.float16
I32 = mybir.dt.int32
ALU = mybir.AluOpType
ACT = mybir.ActivationFunctionType

T = 512
EPS = 1e-5
QUANT = 127.0
X1_SCALE = 2.0 ** 11
H_SCALE = 2.0 ** -1

POOL_STATES = (0, 2, 4, 6, 8, 10, 12, 14)
B_AHEAD = 2
Y_LAG = 2


def mamba_ffn_block(nc, x, w_xproj, w_dt, b_dt, a_log, d_skip, w_gate, w_up, w_down, out):
    BATCH, SEQ, D = x.shape
    N = a_log.shape[1]
    R = w_dt.shape[1]
    HID = w_gate.shape[0]
    DH = D // P
    NH = HID // P
    TT = T // P
    CHUNKS = BATCH * SEQ // T
    BC = 2 * N
    assert DH == 2 and SEQ == 2 * T and CHUNKS >= 4 and N == 16 and NH == 6 and R == 64 and BC == 32
    NP = len(POOL_STATES)
    ND = N - NP
    assert NP % 2 == 0

    x_chunks = x.rearrange("b (h k p) d -> (b h) p k d", p=P, k=TT)
    out_chunks = out.rearrange("b (h k p) d -> (b h) p k d", p=P, k=TT)

    with ExitStack() as ctx:
        def sb(name, shape, dt):
            return ctx.enter_context(nc.sbuf_tensor(name, shape, dt))

        def ps(name, shape):
            return ctx.enter_context(nc.psum_tensor(name, shape, F32))

        def sem(name):
            return ctx.enter_context(nc.semaphore(name))

        ident = sb("ident", [P, P], F32)
        selector = sb("selector", [3 * BC, BC, P], BF16)
        neg_a = sb("neg_a", [P, DH, N], F32)
        a_raw = sb("a_raw", [P, DH, N], F32)
        skip_raw = sb("skip_raw", [P, DH], F32)
        skip1 = sb("skip1", [P, DH], F32)
        skip_diag = sb("skip_diag", [P, DH, P], F32)
        w_xproj_rows = sb("w_xproj_rows", [R + BC, D], F32)
        w_dt_rows = sb("w_dt_rows", [P, DH, R], F32)
        wt_rank = sb("wt_rank", [P, DH, R], F32)
        wt_bc = sb("wt_bc", [P, DH, 3 * BC], F32)
        wt_dt = sb("wt_dt", [R + 1, DH, P], F32)
        w_int = sb("w_int", [P, 3, NH * D], I32)
        w_float = sb("w_float", [P, 3, NH * D], F32)
        wt_gate = sb("wt_gate", [P, DH, HID], F16)
        wt_up = sb("wt_up", [P, DH, HID], F16)
        wt_down = sb("wt_down", [P, NH, D], F16)
        eps_tile = sb("eps_tile", [P, TT], F32)
        neg_half = sb("neg_half", [P, TT], F32)
        neg_one = sb("neg_one", [P, TT], F32)
        x_in = sb("x_in", [P, TT, D], F32)
        x_t = sb("x_t", [P, 2, DH, T], F32)
        rank_t = sb("rank_t", [R + 1, T], F32)
        bc_parts = sb("bc_parts", [3 * BC, 2, T], BF16)
        bc_rest = sb("bc_rest", [3 * BC, T], F32)
        bc_mid = sb("bc_mid", [BC, T], BF16)
        sp_abs = sb("sp_abs", [P, DH, T], F32)
        sp_exp = sb("sp_exp", [P, DH, T], F32)
        sp_log = sb("sp_log", [P, DH, T], F32)
        dt = sb("dt", [P, 2, DH, T], F32)
        u = sb("u", [P, 2, DH, T], F32)
        b_bc = sb("b_bc", [P, 2, T], F32)
        c_bc = sb("c_bc", [P, 2, T], F32)
        ub = sb("ub", [P, 4, DH, T], F32)
        h = sb("h", [P, 4, DH, T], F32)
        h_carry = sb("h_carry", [P, N, DH], F32)
        z = sb("z", [P, DH, T], F32)
        x1 = sb("x1", [P, TT, D], F32)
        x1_t = sb("x1_t", [P, 2, DH, T], F16)
        tanh_g = sb("tanh_g", [P, T], F32)
        silu_g = sb("silu_g", [P, T], F32)
        hid = sb("hid", [P, 2, T], F32)
        hid16 = sb("hid16", [P, 2, NH, T], F16)
        res = sb("res", [P, TT, D], F32)
        res_n = sb("res_n", [P, TT, D], F32)
        stats = sb("stats", [P, 2, TT, 6], F32)
        mean_var = sb("mean_var", [P, 2, TT, 2], F32)
        var_eps = sb("var_eps", [P, 2, TT], F32)
        rstd = sb("rstd", [P, 2, TT], F32)
        neg_mean = sb("neg_mean", [P, 2, TT], F32)
        shift = sb("shift", [P, 2, TT], F32)

        p_da = ps("p_da", [P, DH, T])
        p_y = ps("p_y", [P, DH, T])
        p_b = ps("p_b", [P, T])
        p_c = ps("p_c", [P, T])
        p_m = ps("p_m", [P, 2, T])
        p_m_flat = p_m[:, :, :].rearrange("p a t -> p (a t)")
        p_m_tok = p_m[:, :, :].rearrange("p a (k d) -> p (a k) d", d=D)

        s_small_in = sem("s_small_in")
        s_w_in = sem("s_w_in")
        s_x_in = sem("s_x_in")
        s_out = sem("s_out")
        s_fill = sem("s_fill")
        s_const = sem("s_const")
        s_ones = sem("s_ones")
        s_wfloat = sem("s_wfloat")
        s_wt_ps = sem("s_wt_ps")
        s_wt = sem("s_wt")
        s_a_exp = sem("s_a_exp")
        s_neg_a = sem("s_neg_a")
        s_skip1 = sem("s_skip1")
        s_skip_diag = sem("s_skip_diag")
        s_xt_ps = sem("s_xt_ps")
        s_xt = sem("s_xt")
        s_proj_ps = sem("s_proj_ps")
        s_part1 = sem("s_part1")
        s_rank = sem("s_rank")
        s_rest = sem("s_rest")
        s_part2 = sem("s_part2")
        s_parts = sem("s_parts")
        s_dt_ps = sem("s_dt_ps")
        s_sp_abs = sem("s_sp_abs")
        s_sp_exp = sem("s_sp_exp")
        s_sp_log = sem("s_sp_log")
        s_dt = sem("s_dt")
        s_u = sem("s_u")
        s_b_ps = sem("s_b_ps")
        s_b = sem("s_b")
        s_ub = sem("s_ub")
        s_da = sem("s_da")
        s_scan = sem("s_scan")
        s_carry = sem("s_carry")
        s_c_ps = sem("s_c_ps")
        s_c = sem("s_c")
        s_hc_dve = sem("s_hc_dve")
        s_hc_pool = sem("s_hc_pool")
        s_y = sem("s_y")
        s_z = sem("s_z")
        s_zt_ps = sem("s_zt_ps")
        s_stats = sem("s_stats")
        s_mean = sem("s_mean")
        s_ln_a = sem("s_ln_a")
        s_ln_b = sem("s_ln_b")
        s_ln = sem("s_ln")
        s_x1 = sem("s_x1")
        s_x1t_ps = sem("s_x1t_ps")
        s_x1_hi = sem("s_x1_hi")
        s_x1_lo = sem("s_x1_lo")
        s_gu_ps = sem("s_gu_ps")
        s_tanh = sem("s_tanh")
        s_silu = sem("s_silu")
        s_hid = sem("s_hid")
        s_hid_hi = sem("s_hid_hi")
        s_hid_lo = sem("s_hid_lo")
        s_o_ps = sem("s_o_ps")
        s_res = sem("s_res")
        s_out_ready = sem("s_out_ready")

        block = ctx.enter_context(nc.Block())

        def wait(eng, s, value):
            if not isinstance(value, int) or value > 0:
                eng.wait_ge(s, value)

        def units(c, s):
            return N * c + (s + 1)

        def wait_hc(eng, c, s):
            if s in POOL_STATES:
                wait(eng, s_hc_pool, NP * c + (POOL_STATES.index(s) + 1))
            else:
                wait(eng, s_hc_dve, ND * c + (sum(q not in POOL_STATES for q in range(s)) + 1))

        def wait_c_read(eng, c, s):
            if s in POOL_STATES:
                wait(eng, s_c, NP * c + (POOL_STATES.index(s) + 1))
            else:
                wait_hc(eng, c, s)

        def unit_at(c, s, k, par):
            if s + k < 0:
                return c - 1, s + k + N, 1 - par
            if s + k >= N:
                return c + 1, s + k - N, 1 - par
            return c, s + k, par

        def over_chunks(eng, step):
            step(0, 0, 0, False, True, True)
            with eng.Fori(0, CHUNKS // 2 - 1) as i:
                step(2 * i + 1, 1, i, True, True, True)
                step(2 * i + 2, 0, i + 1, True, True, True)
            step(CHUNKS - 1, 1, CHUNKS // 2 - 1, True, True, False)
            step(CHUNKS, 0, CHUNKS // 2, True, False, False)

        SMALL_LOADS = 6

        @block.sync
        def _(sp):
            sp.sem_inc(s_out, 16)
            sp.dma_start(x_in[:, :, :], x_chunks[0]).then_inc(s_x_in, 16)
            sp.dma_start(w_xproj_rows[:, :], w_xproj).then_inc(s_small_in, 16)
            sp.dma_start(w_dt_rows[:, :, :], w_dt.rearrange("(h p) r -> p h r", p=P)).then_inc(s_small_in, 16)
            sp.dma_start(wt_dt[R:R + 1, :, :],
                         b_dt.rearrange("(a h p) -> a h p", a=1, p=P)).then_inc(s_small_in, 16)
            sp.dma_start(a_raw[:, :, :], a_log.rearrange("(h p) n -> p h n", p=P)).then_inc(s_small_in, 16)
            for q in range(DH):
                sp.dma_start(skip_raw[:, q:q + 1],
                             d_skip[q * P:(q + 1) * P].rearrange("(p a) -> p a", a=1)).then_inc(s_small_in, 16)
            sp.dma_start(w_int[:, 0, :].rearrange("p (j d) -> p j d", d=D),
                         w_gate.rearrange("(j p) d -> p j d", p=P)).then_inc(s_w_in, 16)
            sp.dma_start(w_int[:, 1, :].rearrange("p (j d) -> p j d", d=D),
                         w_up.rearrange("(j p) d -> p j d", p=P)).then_inc(s_w_in, 16)
            sp.dma_start(w_int[:, 2, :].rearrange("p (q f) -> p q f", q=DH),
                         w_down.rearrange("(q p) f -> p q f", p=P)).then_inc(s_w_in, 16)
            wait(sp, s_xt_ps, 1)
            sp.dma_start(x_in[:, :, :], x_chunks[1]).then_inc(s_x_in, 16)

            def store(c):
                wait(sp, s_out_ready, c + 1)
                sp.dma_start(out_chunks[bass.ds(c, 1)].rearrange("a p k d -> (a p) k d"),
                             res_n[:, :, :]).then_inc(s_out, 16)

            def load(c):
                wait(sp, s_xt_ps, c)
                sp.dma_start(x_in[:, :, :],
                             x_chunks[bass.ds(c, 1)].rearrange("a p k d -> (a p) k d")).then_inc(s_x_in, 16)

            with sp.Fori(0, CHUNKS - 2) as i:
                load(i + 2)
                store(i)
            store(CHUNKS - 2)
            store(CHUNKS - 1)
            sp.wait_ge(s_out, 16 * (CHUNKS + 1))

        @block.gpsimd
        def _(pool):
            nc.gpsimd.memset(ident[:, :], 0.0).then_inc(s_fill, 1)
            nc.gpsimd.memset(selector[:, :, :], 0.0).then_inc(s_fill, 1)
            nc.gpsimd.memset(eps_tile[:, :], EPS)
            nc.gpsimd.memset(neg_half[:, :], -0.5)
            nc.gpsimd.memset(neg_one[:, :], -1.0)
            pool.wait_ge(s_fill, 2)
            nc.gpsimd.affine_select(out=ident[:, :], in_=ident[:, :], compare_op=ALU.not_equal, fill=1.0,
                                    base=0, pattern=[[-1, P]], channel_multiplier=1).then_inc(s_const, 1)
            for part in range(3):
                pool.wait_ge(s_const, part + 1)
                nc.gpsimd.affine_select(out=selector[:, :, :], in_=selector[:, :, :], compare_op=ALU.not_equal,
                                        fill=1.0, base=-BC * part, pattern=[[-1, BC], [0, P]],
                                        channel_multiplier=1).then_inc(s_const, 1)

            def third_part(c, par):
                wait(pool, s_part2, 2 * (c + 1))
                nc.gpsimd.tensor_tensor(bc_parts[0:BC, par, :], bc_rest[0:BC, :], bc_mid[:, :],
                                        ALU.subtract).then_inc(s_parts, 1)

            def u_of(c, par):
                wait(pool, s_dt, c + 1)
                nc.gpsimd.tensor_tensor(u[:, par, :, :], dt[:, par, :, :], x_t[:, par, :, :],
                                        ALU.mult).then_inc(s_u, 1)

            def times_b(c, s, par):
                wait(pool, s_u, c + 1)
                wait(pool, s_b, units(c, s))
                wait(pool, s_scan, 2 * units(c, s) - 2 * 4)
                nc.gpsimd.tensor_tensor(ub[:, s % 4, :, :], u[:, par, :, :],
                                        b_bc[:, s % 2:s % 2 + 1, :].broadcast_to([P, DH, T]),
                                        ALU.mult).then_inc(s_ub, 1)

            def times_c(c, s, par, batch):
                i = POOL_STATES.index(s)
                wait(pool, s_c, NP * c + (i + 1))
                wait(pool, s_scan, 2 * units(c, s))
                if par == 0:
                    wait(pool, s_carry, units(batch, s))
                nc.gpsimd.tensor_tensor(h[:, s % 4, :, :], h[:, s % 4, :, :],
                                        c_bc[:, i % 2:i % 2 + 1, :].broadcast_to([P, DH, T]),
                                        ALU.mult).then_inc(s_hc_pool, 1)

            def norm_scalars(k, done, count):
                wait(pool, s_mean, count)
                nc.gpsimd.tensor_tensor(var_eps[:, k, :], mean_var[:, k, :, 1], eps_tile[:, :],
                                        ALU.add).then_inc(s_ln_a, 1)
                nc.gpsimd.tensor_tensor(neg_mean[:, k, :], mean_var[:, k, :, 0], neg_one[:, :],
                                        ALU.mult).then_inc(s_ln_a, 1)
                wait(pool, s_ln_a, 2 * count)
                nc.gpsimd.tensor_tensor(rstd[:, k, :], var_eps[:, k, :], neg_half[:, :],
                                        ALU.pow).then_inc(s_ln_b, 1)
                wait(pool, s_ln_b, count)
                nc.gpsimd.tensor_tensor(shift[:, k, :], neg_mean[:, k, :], rstd[:, k, :],
                                        ALU.mult).then_inc(s_ln, 1)

            def low_half(c, j):
                wait(pool, s_hid_hi, NH * c + (j + 1))
                nc.gpsimd.tensor_tensor(hid16[:, 1, j, :], hid[:, j % 2, :], hid16[:, 0, j, :],
                                        ALU.subtract).then_inc(s_hid_lo, 1)

            third_part(0, 0)
            u_of(0, 0)
            for s in range(B_AHEAD):
                times_b(0, s, 0)

            def step(c, par, batch, prev, core, nxt):
                for s in range(N):
                    if core:
                        ca, sa, pa = unit_at(c, s, B_AHEAD, par)
                        if sa >= B_AHEAD or nxt:
                            times_b(ca, sa, pa)
                    if prev and s == 3:
                        norm_scalars(0, s_ln, 2 * (c - 1) + 1)
                    if prev and s == 15:
                        norm_scalars(1, s_ln, 2 * (c - 1) + 2)
                    if nxt and s == 3:
                        third_part(c + 1, 1 - par)
                    if nxt and s == 6:
                        u_of(c + 1, 1 - par)
                    if prev and 8 <= s < 8 + NH:
                        low_half(c - 1, s - 8)
                    cb, sb_, pb = unit_at(c, s, -1, par)
                    if (core and s > 0 or prev and s == 0) and sb_ in POOL_STATES:
                        times_c(cb, sb_, pb, batch)
            over_chunks(pool, step)

        @block.scalar
        def _(act):
            act.wait_ge(s_small_in, 16 * SMALL_LOADS)
            nc.scalar.activation(neg_a[:, :, :], a_raw[:, :, :], ACT.Exp).then_inc(s_a_exp, 1)
            act.wait_ge(s_wt_ps, 1)
            nc.scalar.copy(wt_rank[:, :, :], p_m[:, 0, 0:DH * (R + BC)].rearrange(
                "p (q r) -> p q r", q=DH)[:, :, 0:R]).then_inc(s_wt, 1)
            for part in range(3):
                nc.scalar.copy(wt_bc[:, :, part * BC:(part + 1) * BC],
                               p_m[:, 0, 0:DH * (R + BC)].rearrange(
                                   "p (q r) -> p q r", q=DH)[:, :, R:R + BC]).then_inc(s_wt, 1)
            nc.scalar.copy(wt_dt[0:R, :, :], p_m[0:R, 1, 0:DH * P].rearrange(
                "p (q r) -> p q r", q=DH)).then_inc(s_wt, 1)
            act.wait_ge(s_neg_a, 1)
            act.wait_ge(s_skip1, 1)
            act.wait_ge(s_const, 1)
            for q in range(DH):
                nc.scalar.mul(skip_diag[:, q, :], ident[:, :], skip1[:, q:q + 1]).then_inc(s_skip_diag, 1)
            dsts = ([wt_gate[:, q, :] for q in range(DH)] + [wt_up[:, q, :] for q in range(DH)]
                    + [wt_down[:, 3 * q:3 * q + 3, :].rearrange("p j d -> p (j d)") for q in range(2)])
            for n, dst in enumerate(dsts):
                act.wait_ge(s_wt_ps, n + 2)
                nc.scalar.copy(dst, p_m_flat[:, 0:HID]).then_inc(s_wt, 1)

            def x_out(c, par):
                wait(act, s_xt_ps, c + 1)
                nc.scalar.copy(x_t[:, par, :, :], p_m[:, :, :]).then_inc(s_xt, 1)

            def proj_out(c, par):
                wait(act, s_proj_ps, c + 1)
                nc.scalar.copy(rank_t[0:R, :], p_m[0:R, 1, :]).then_inc(s_rank, 1)
                nc.scalar.copy(bc_parts[:, par, :], p_m[0:3 * BC, 0, :]).then_inc(s_part1, 1)

            def second_parts(c, par):
                wait(act, s_rest, c + 1)
                nc.scalar.copy(bc_parts[BC:2 * BC, par, :], bc_rest[BC:2 * BC, :]).then_inc(s_part2, 1)
                nc.scalar.copy(bc_mid[:, :], bc_rest[0:BC, :]).then_inc(s_part2, 1)

            def softplus(c):
                wait(act, s_dt_ps, c + 1)
                nc.scalar.activation(sp_abs[:, :, :], p_m[:, :, :], ACT.Abs).then_inc(s_sp_abs, 1)
                wait(act, s_sp_abs, c + 1)
                nc.scalar.activation(sp_exp[:, :, :], sp_abs[:, :, :], ACT.Exp, scale=-1.0).then_inc(s_sp_exp, 1)
                wait(act, s_sp_exp, c + 1)
                nc.scalar.activation(sp_log[:, :, :], sp_exp[:, :, :], ACT.Ln, bias=1.0).then_inc(s_sp_log, 1)

            def b_out(c, s):
                wait(act, s_b_ps, units(c, s))
                wait(act, s_ub, units(c, s) - 2)
                nc.scalar.copy(b_bc[:, s % 2, :], p_b[:, :]).then_inc(s_b, 1)

            def c_out(c, s):
                i = POOL_STATES.index(s)
                wait(act, s_c_ps, units(c, s))
                wait(act, s_hc_pool, NP * c + (i + 1) - 2)
                nc.scalar.copy(c_bc[:, i % 2, :], p_c[:, :]).then_inc(s_c, 1)

            def decay(c, s, par, q):
                wait(act, s_dt, c + 1)
                wait(act, s_scan, 2 * units(c, s) - 2 + q - 1)
                nc.scalar.activation(p_da[:, q, :], dt[:, par, q, :], ACT.Exp,
                                     scale=neg_a[:, q, s:s + 1]).then_inc(s_da, 1)

            def z_out(c):
                wait(act, s_y, N * (c + 1))
                nc.scalar.copy(z[:, :, :], p_y[:, :, :]).then_inc(s_z, 1)

            def norm1(c):
                wait(act, s_zt_ps, c + 1)
                wait(act, s_ln, 2 * c + 1)
                for k in range(TT):
                    nc.scalar.activation(x1[:, k, :], p_m_tok[:, k, :], ACT.Identity, bias=shift[:, 0, k:k + 1],
                                         scale=rstd[:, 0, k:k + 1]).then_inc(s_x1, 1)

            def x1_high(c):
                wait(act, s_x1t_ps, c + 1)
                nc.scalar.mul(x1_t[:, 0, :, :], p_m[:, :, :], X1_SCALE).then_inc(s_x1_hi, 1)

            def tanh_of(c, j):
                wait(act, s_gu_ps, NH * c + (j + 1))
                nc.scalar.activation(tanh_g[:, :], p_m[:, 0, :], ACT.Tanh,
                                     scale=0.5 / (QUANT * X1_SCALE)).then_inc(s_tanh, 1)

            def high_half(c, j):
                wait(act, s_hid, NH * c + (j + 1))
                nc.scalar.copy(hid16[:, 0, j, :], hid[:, j % 2, :]).then_inc(s_hid_hi, 1)

            def norm2(c):
                wait(act, s_ln, 2 * c + 2)
                wait(act, s_res, 2 * (c + 1))
                wait(act, s_out, 16 * (c + 1))
                for k in range(TT):
                    ins = nc.scalar.activation(res_n[:, k, :], res[:, k, :], ACT.Identity,
                                               bias=shift[:, 1, k:k + 1], scale=rstd[:, 1, k:k + 1])
                ins.then_inc(s_out_ready, 1)

            x_out(0, 0)
            proj_out(0, 0)
            second_parts(0, 0)
            softplus(0)
            for s in range(B_AHEAD):
                b_out(0, s)
            for q in range(DH):
                decay(0, 0, 0, q)

            def step(c, par, batch, prev, core, nxt):
                for s in range(N):
                    cb, sb_, _ = unit_at(c, s, -1, par)
                    if (core and s > 0 or prev and s == 0) and sb_ in POOL_STATES:
                        c_out(cb, sb_)
                    if core:
                        ca, sa, _ = unit_at(c, s, B_AHEAD, par)
                        if sa >= B_AHEAD or nxt:
                            b_out(ca, sa)
                        ce, se, pe_ = unit_at(c, s, 1, par)
                        if se > 0 or nxt:
                            for q in range(DH):
                                decay(ce, se, pe_, q)
                    if nxt and s == 0:
                        x_out(c + 1, 1 - par)
                    if prev and s == 1:
                        z_out(c - 1)
                    if nxt and s == 1:
                        proj_out(c + 1, 1 - par)
                    if nxt and s == 2:
                        second_parts(c + 1, 1 - par)
                    if prev and s == 3:
                        norm1(c - 1)
                    if prev and s == 4:
                        x1_high(c - 1)
                    if nxt and s == 5:
                        softplus(c + 1)
                    if prev and 7 <= s < 7 + NH:
                        high_half(c - 1, s - 7)
                    if prev and 6 <= s < 6 + NH:
                        tanh_of(c - 1, s - 6)
                    if prev and s == 15:
                        norm2(c - 1)
            over_chunks(act, step)

        @block.vector
        def _(dve):
            nc.vector.memset(rank_t[R:R + 1, :], 1.0).then_inc(s_ones, 1)
            dve.wait_ge(s_a_exp, 1)
            nc.vector.tensor_scalar_mul(neg_a[:, :, :], neg_a[:, :, :], -1.0).then_inc(s_neg_a, 1)
            nc.vector.tensor_scalar_add(skip1[:, :], skip_raw[:, :], 1.0).then_inc(s_skip1, 1)
            dve.wait_ge(s_w_in, 16 * 3)
            for n in range(3):
                nc.vector.tensor_copy(w_float[:, n, :], w_int[:, n, :]).then_inc(s_wfloat, 1)

            def rest(c, par):
                wait(dve, s_proj_ps, c + 1)
                wait(dve, s_part1, c + 1)
                nc.vector.tensor_tensor(bc_rest[:, :], p_m[0:3 * BC, 0, :], bc_parts[:, par, :],
                                        ALU.subtract).then_inc(s_rest, 1)

            def dt_of(c, par):
                wait(dve, s_sp_log, c + 1)
                nc.vector.scalar_tensor_tensor(dt[:, par, :, :], p_m[:, :, :], 0.0, sp_log[:, :, :],
                                               ALU.max, ALU.add).then_inc(s_dt, 1)

            def scan(c, s, par, batch, q):
                wait(dve, s_da, 2 * units(c, s) - 1 + q)
                if q == 0:
                    wait(dve, s_ub, units(c, s))
                    wait(dve, s_y, units(c, s) - 4)
                if par == 0:
                    initial = 0.0
                else:
                    initial = h_carry[:, s, q:q + 1]
                    if q == 0:
                        wait(dve, s_carry, units(batch, s))
                nc.vector.tensor_tensor_scan(h[:, s % 4, q, :], p_da[:, q, :], ub[:, s % 4, q, :], initial,
                                             ALU.mult, ALU.add).then_inc(s_scan, 1)

            def carry(c, s):
                wait(dve, s_scan, 2 * units(c, s))
                nc.vector.tensor_copy(h_carry[:, s, :], h[:, s % 4, :, T - 1]).then_inc(s_carry, 1)

            def times_c(c, s, par, batch):
                wait(dve, s_c_ps, units(c, s))
                wait(dve, s_scan, 2 * units(c, s))
                if par == 0:
                    wait(dve, s_carry, units(batch, s))
                nc.vector.tensor_tensor(h[:, s % 4, :, :], h[:, s % 4, :, :],
                                        p_c[:, :].rearrange("p (a t) -> p a t", a=1).broadcast_to([P, DH, T]),
                                        ALU.mult).then_inc(s_hc_dve, 1)

            def norm_stats(k, src):
                for t in range(TT):
                    nc.vector.bn_stats(stats[:, k, t, :], src[:, t, :]).then_inc(s_stats, 1)

            def norm_mean(k):
                for t in range(TT):
                    ins = nc.vector.bn_aggr(mean_var[:, k, t, :], stats[:, k, t, :])
                ins.then_inc(s_mean, 1)

            def x1_low(c):
                wait(dve, s_x1_hi, c + 1)
                nc.vector.scalar_tensor_tensor(x1_t[:, 1, :, :], p_m[:, :, :], X1_SCALE, x1_t[:, 0, :, :],
                                               ALU.mult, ALU.subtract).then_inc(s_x1_lo, 1)

            def silu_of(c, j):
                wait(dve, s_tanh, NH * c + (j + 1))
                nc.vector.scalar_tensor_tensor(silu_g[:, :], tanh_g[:, :], 1.0, p_m[:, 0, :],
                                               ALU.add, ALU.mult).then_inc(s_silu, 1)

            def hidden(c, j):
                wait(dve, s_silu, NH * c + (j + 1))
                if j >= 2:
                    wait(dve, s_hid_lo, NH * c + (j - 1))
                nc.vector.scalar_tensor_tensor(hid[:, j % 2, :], p_m[:, 1, :],
                                               H_SCALE / (2.0 * QUANT * QUANT * X1_SCALE * X1_SCALE),
                                               silu_g[:, :], ALU.mult, ALU.mult).then_inc(s_hid, 1)

            def residual(c):
                for a in range(2):
                    wait(dve, s_o_ps, 2 * c + (a + 1))
                    nc.vector.scalar_tensor_tensor(
                        res[:, 2 * a:2 * a + 2, :], p_m_tok[:, 2 * a:2 * a + 2, :], 1.0 / (QUANT * H_SCALE),
                        x1[:, 2 * a:2 * a + 2, :], ALU.mult, ALU.add).then_inc(s_res, 1)

            rest(0, 0)
            dt_of(0, 0)

            def step(c, par, batch, prev, core, nxt):
                for s in range(N):
                    if nxt and s == 2:
                        rest(c + 1, 1 - par)
                    if prev and s == 3:
                        wait(dve, s_zt_ps, c)
                        norm_stats(0, p_m_tok)
                    if prev and s == 5:
                        x1_low(c - 1)
                    if nxt and s == 6:
                        dt_of(c + 1, 1 - par)
                    if prev and s == 15:
                        residual(c - 1)
                    if core:
                        scan(c, s, par, batch, 0)
                    cb, sb_, pb = unit_at(c, s, -1, par)
                    last_unit = core and s > 0 or prev and s == 0
                    if last_unit and pb == 0:
                        carry(cb, sb_)
                    if prev and s == 15:
                        wait(dve, s_res, 2 * c)
                        norm_stats(1, res)
                    if prev and s in (3, 15):
                        wait(dve, s_stats, TT * (2 * (c - 1) + (1 if s == 3 else 2)))
                    if core:
                        scan(c, s, par, batch, 1)
                    if prev and s in (3, 15):
                        norm_mean(0 if s == 3 else 1)
                    if prev and 7 <= s < 7 + NH:
                        silu_of(c - 1, s - 7)
                    if last_unit and sb_ not in POOL_STATES:
                        times_c(cb, sb_, pb, batch)
                    if prev and 7 <= s < 7 + NH:
                        hidden(c - 1, s - 7)
            over_chunks(dve, step)

        @block.tensor
        def _(pe):
            pe.wait_ge(s_const, 4)
            pe.wait_ge(s_small_in, 16 * SMALL_LOADS)
            for q in range(DH):
                nc.tensor.transpose(p_m[:, 0, q * (R + BC):(q + 1) * (R + BC)],
                                    w_xproj_rows[:, q * P:(q + 1) * P], ident[0:R + BC, 0:R + BC])
            for q in range(DH):
                ins = nc.tensor.transpose(p_m[0:R, 1, q * P:(q + 1) * P], w_dt_rows[:, q, :], ident[:, :])
            ins.then_inc(s_wt_ps, 1)
            pe.wait_ge(s_wt, 5)
            w_tiles = [w_float[:, n, :].rearrange("p (j d) -> p j d", d=D) for n in range(2)]
            w_down_tiles = w_float[:, 2, :].rearrange("p (q f) -> p q f", q=DH)
            pe.wait_ge(s_wfloat, 3)
            for n in range(4):
                if n:
                    pe.wait_ge(s_wt, 5 + n)
                for j in range(NH):
                    ins = nc.tensor.transpose(p_m_flat[:, j * P:(j + 1) * P],
                                              w_tiles[n // DH][:, j, (n % DH) * P:(n % DH + 1) * P], ident[:, :])
                ins.then_inc(s_wt_ps, 1)
            for n in range(2):
                pe.wait_ge(s_wt, 9 + n)
                for j in range(3):
                    for q in range(DH):
                        ins = nc.tensor.transpose(
                            p_m_flat[:, (DH * j + q) * P:(DH * j + q + 1) * P],
                            w_down_tiles[:, q, (3 * n + j) * P:(3 * n + j + 1) * P], ident[:, :])
                ins.then_inc(s_wt_ps, 1)
            pe.wait_ge(s_wt, 11)

            def x_transposed(c):
                wait(pe, s_x_in, 16 * (c + 1))
                wait(pe, s_scan, 2 * N * (c - 1))
                if isinstance(c, int) and c == 1:
                    wait(pe, s_dt, 1)
                for q in range(DH):
                    for k in range(TT):
                        ins = nc.tensor.transpose(p_m[:, q, k * P:(k + 1) * P],
                                                  x_in[:, k, q * P:(q + 1) * P], ident[:, :])
                ins.then_inc(s_xt_ps, 1)

            def project(c, par):
                wait(pe, s_xt, c + 1)
                for q in range(DH):
                    nc.tensor.matmul(p_m[0:R, 1, :], wt_rank[:, q, :], x_t[:, par, q, :],
                                     start=(q == 0), stop=(q == DH - 1))
                for q in range(DH):
                    ins = nc.tensor.matmul(p_m[0:3 * BC, 0, :], wt_bc[:, q, :], x_t[:, par, q, :],
                                           start=(q == 0), stop=(q == DH - 1))
                ins.then_inc(s_proj_ps, 1)

            def project_dt(c):
                wait(pe, s_rank, c + 1)
                wait(pe, s_rest, c + 1)
                for q in range(DH):
                    ins = nc.tensor.matmul(p_m[:, q, :], wt_dt[:, q, :], rank_t[:, :], start=True, stop=True)
                ins.then_inc(s_dt_ps, 1)

            def broadcast_b(c, s, par):
                wait(pe, s_parts, c + 1)
                wait(pe, s_b, units(c, s) - 1)
                nc.tensor.matmul(p_b[:, :], selector[:, s, :], bc_parts[:, par, :],
                                 start=True, stop=True).then_inc(s_b_ps, 1)

            def broadcast_c(c, s, par):
                cb, sb_, _ = unit_at(c, s, -1, par)
                if not (isinstance(cb, int) and cb < 0):
                    wait_c_read(pe, cb, sb_)
                nc.tensor.matmul(p_c[:, :], selector[:, N + s, :], bc_parts[:, par, :],
                                 start=True, stop=True).then_inc(s_c_ps, 1)

            def sum_states(c, s, par):
                if s == 0:
                    wait(pe, s_z, c)
                    for q in range(DH):
                        nc.tensor.matmul(p_y[:, q, :], skip_diag[:, q, :], x_t[:, par, q, :],
                                         start=True, stop=False)
                wait_hc(pe, c, s)
                for q in range(DH):
                    ins = nc.tensor.matmul(p_y[:, q, :], ident[:, :], h[:, s % 4, q, :],
                                           start=False, stop=(s == N - 1))
                ins.then_inc(s_y, 1)

            def z_transposed(c):
                wait(pe, s_z, c + 1)
                for k in range(TT):
                    for q in range(DH):
                        ins = nc.tensor.transpose(p_m_tok[:, k, q * P:(q + 1) * P],
                                                  z[:, q, k * P:(k + 1) * P], ident[:, :])
                ins.then_inc(s_zt_ps, 1)

            def x1_transposed(c):
                wait(pe, s_x1, TT * (c + 1))
                for q in range(DH):
                    for k in range(TT):
                        ins = nc.tensor.transpose(p_m[:, q, k * P:(k + 1) * P],
                                                  x1[:, k, q * P:(q + 1) * P], ident[:, :])
                ins.then_inc(s_x1t_ps, 1)

            def gate_up(c, j):
                if j == 0:
                    wait(pe, s_x1_lo, c + 1)
                else:
                    wait(pe, s_hid, NH * c + j)
                for a, w in enumerate((wt_gate, wt_up)):
                    for n in range(2 * DH):
                        ins = nc.tensor.matmul(p_m[:, a, :], w[:, n % DH, j * P:(j + 1) * P],
                                               x1_t[:, n // DH, n % DH, :],
                                               start=(n == 0), stop=(n == 2 * DH - 1))
                ins.then_inc(s_gu_ps, 1)

            def down(c):
                wait(pe, s_hid_lo, NH * (c + 1))
                for k in range(TT):
                    for n in range(2 * NH):
                        ins = nc.tensor.matmul(p_m_tok[:, k, :], hid16[:, n // NH, n % NH, k * P:(k + 1) * P],
                                               wt_down[:, n % NH, :], start=(n == 0), stop=(n == 2 * NH - 1))
                    if k % 2:
                        ins.then_inc(s_o_ps, 1)

            x_transposed(0)
            project(0, 0)
            pe.wait_ge(s_ones, 1)
            project_dt(0)
            for s in range(B_AHEAD):
                broadcast_b(0, s, 0)

            def step(c, par, batch, prev, core, nxt):
                for s in range(N):
                    cy, sy, py = unit_at(c, s, -Y_LAG, par)
                    if core and s >= Y_LAG or prev and s < Y_LAG:
                        sum_states(cy, sy, py)
                    if core:
                        ca, sa, pa = unit_at(c, s, B_AHEAD, par)
                        if sa >= B_AHEAD or nxt:
                            broadcast_b(ca, sa, pa)
                        broadcast_c(c, s, par)
                    if nxt and s == 0:
                        x_transposed(c + 1)
                    if nxt and s == 1:
                        project(c + 1, 1 - par)
                    if prev and s == 2:
                        if nxt:
                            wait(pe, s_rank, c + 2)
                            wait(pe, s_rest, c + 2)
                        z_transposed(c - 1)
                    if prev and s == 4:
                        x1_transposed(c - 1)
                    if nxt and s == 5:
                        if prev:
                            wait(pe, s_x1_lo, c)
                        project_dt(c + 1)
                    if prev and 6 <= s < 6 + NH:
                        if nxt and s == 6:
                            wait(pe, s_dt, c + 2)
                        gate_up(c - 1, s - 6)
                    if prev and s == 14:
                        down(c - 1)
            over_chunks(pe, step)


_INS = ['L0_attn_x', 'L0_attn_W_xproj', 'L0_attn_W_dt', 'L0_attn_b_dt', 'L0_attn_A_log', 'L0_attn_Dp',
        'L0_ffn_w_gate', 'L0_ffn_w_up', 'L0_ffn_w_down']


def kernel(**inputs):
    import numpy as _np
    import concourse.bacc as _bacc
    from concourse import mybir as _mybir
    from concourse.bass_utils import run_bass_kernel_spmd as _run

    nc = _bacc.Bacc("TRN2", target_bir_lowering=False, num_devices=1)
    arrays, args = {}, []
    for name in _INS:
        a = _np.ascontiguousarray(inputs[name])
        arrays[f"in_{name}"] = a
        args.append(nc.dram_tensor(f"in_{name}", a.shape, _mybir.dt.from_np(a.dtype), kind="ExternalInput").ap())
    out = nc.dram_tensor("out_x", inputs['L0_attn_x'].shape, _mybir.dt.float32, kind="ExternalOutput").ap()
    mamba_ffn_block(nc, *args, out)
    r = _run(nc, [arrays], core_ids=[0])
    return r.results[0]["out_x"]
```

```python
from contextlib import ExitStack

import concourse.bass as bass
from concourse import mybir

P = 128
F32 = mybir.dt.float32
BF16 = mybir.dt.bfloat16
F16 = mybir.dt.float16
I32 = mybir.dt.int32
ALU = mybir.AluOpType
ACT = mybir.ActivationFunctionType

T = 512
EPS = 1e-5
QUANT = 127.0
X1_SCALE = 2.0 ** 11
H_SCALE = 2.0 ** -1

POOL_STATES = (0, 1, 3, 5, 7, 10)

UB_AHEAD = 3
DA_AHEAD = 1
POOL_LAG = 2
SUM_LAG = {True: 4, False: 2}

B_GROUP = 4
UB_SLOTS = 4
H_SLOTS = 8


def mamba_ffn_block(nc, x, w_xproj, w_dt, b_dt, a_log, d_skip, w_gate, w_up, w_down, out):
    BATCH, SEQ, D = x.shape
    N = a_log.shape[1]
    R = w_dt.shape[1]
    HID = w_gate.shape[0]
    DH = D // P
    NH = HID // P
    TT = T // P
    CHUNKS = BATCH * SEQ // T
    BC = 2 * N
    assert DH == 2 and SEQ == 2 * T and CHUNKS >= 4 and N == 16 and NH == 6 and R == 64 and BC == 32
    NP = len(POOL_STATES)
    ND = N - NP
    DVE_STATES = [s for s in range(N) if s not in POOL_STATES]
    POOL_RUNS = []
    for s in POOL_STATES:
        if POOL_RUNS and POOL_RUNS[-1][-1] == s - 1:
            POOL_RUNS[-1].append(s)
        else:
            POOL_RUNS.append([s])
    assert ND % 2 == 0 and N % B_GROUP == N % UB_SLOTS == N % H_SLOTS == 0
    sum_at = {s: s + SUM_LAG[s in POOL_STATES] for s in range(N)}
    SUM_ORDER = sorted(range(N), key=lambda s: (sum_at[s], s))
    assert all(sum_at[s] < N or s not in POOL_STATES for s in range(N))

    x_chunks = x.rearrange("b (h k p) d -> (b h) p k d", p=P, k=TT)
    out_chunks = out.rearrange("b (h k p) d -> (b h) p k d", p=P, k=TT)

    with ExitStack() as ctx:
        def sb(name, shape, dt):
            return ctx.enter_context(nc.sbuf_tensor(name, shape, dt))

        def ps(name, shape):
            return ctx.enter_context(nc.psum_tensor(name, shape, F32))

        def sem(name):
            return ctx.enter_context(nc.semaphore(name))

        ident = sb("ident", [P, P], F32)
        selector = sb("selector", [3 * BC, N, P], BF16)
        neg_a = sb("neg_a", [P, DH, N], F32)
        a_raw = sb("a_raw", [P, DH, N], F32)
        skip_raw = sb("skip_raw", [P, DH], F32)
        skip1 = sb("skip1", [P, DH], F32)
        skip_diag = sb("skip_diag", [P, DH, P], F32)
        w_xproj_rows = sb("w_xproj_rows", [R + BC, D], F32)
        w_dt_rows = sb("w_dt_rows", [P, DH, R], F32)
        wt_rank = sb("wt_rank", [P, DH, R], F32)
        wt_bc = sb("wt_bc", [P, DH, 3 * BC], F32)
        wt_dt = sb("wt_dt", [R + 1, DH, P], F32)
        wt_gate = sb("wt_gate", [P, DH, HID], F16)
        wt_up = sb("wt_up", [P, DH, HID], F16)
        wt_down = sb("wt_down", [P, NH, D], F16)
        eps_tile = sb("eps_tile", [P, TT], F32)
        neg_half = sb("neg_half", [P, TT], F32)
        neg_one = sb("neg_one", [P, TT], F32)
        x_in = sb("x_in", [P, TT, D], F32)
        x_t = sb("x_t", [P, 2, DH, T], F32)
        rank_t = sb("rank_t", [R + 1, T], F32)
        bc_rows = sb("bc_rows", [BC, T], F32)
        bc_parts = sb("bc_parts", [3 * BC, 2, T], BF16)
        bc_rest = sb("bc_rest", [3 * BC, T], F32)
        bc_mid = sb("bc_mid", [BC, T], BF16)
        sp_abs = sb("sp_abs", [P, DH, T], F32)
        sp_relu = sb("sp_relu", [P, DH, T], F32)
        dt = sb("dt", [P, 2, DH, T], F32)
        u = sb("u", [P, 2, DH, T], F32)
        b_bc = sb("b_bc", [P, N, T], F32)
        c_bc = sb("c_bc", [P, NP, T], F32)
        ub = sb("ub", [P, UB_SLOTS, DH, T], F32)
        h = sb("h", [P, H_SLOTS, DH, T], F32)
        ring_h = h[:, :, :, :].rearrange("p a q t -> p (a q t)")
        ring_ub = ub[:, :, :, :].rearrange("p a q t -> p (a q t)")
        w_float = [ring_h[:, n * NH * D:(n + 1) * NH * D] for n in range(3)]
        w_int = [ring_h[:, n * NH * D:(n + 1) * NH * D].bitcast(I32) for n in range(3, 5)]
        w_int.append(ring_ub[:, 0:NH * D].bitcast(I32))
        h_carry = sb("h_carry", [P, N, DH], F32)
        z = sb("z", [P, DH, T], F32)
        x1 = sb("x1", [P, TT, D], F32)
        x1_t = sb("x1_t", [P, 2, DH, T], F16)
        tanh_g = sb("tanh_g", [P, T], F32)
        silu_g = sb("silu_g", [P, T], F32)
        hid = sb("hid", [P, 2, T], F32)
        hid16 = sb("hid16", [P, 2, NH, T], F16)
        res = sb("res", [P, TT, D], F32)
        res_n = sb("res_n", [P, TT, D], F32)
        stats = sb("stats", [P, 2, TT, 6], F32)
        mean_var = sb("mean_var", [P, 2, TT, 2], F32)
        var_eps = sb("var_eps", [P, 2, TT], F32)
        rstd = sb("rstd", [P, 2, TT], F32)
        neg_mean = sb("neg_mean", [P, 2, TT], F32)
        shift = sb("shift", [P, 2, TT], F32)

        bc_dram = nc.dram_tensor("bc_rows_dram", (2, BC, T), F32, kind="Internal").ap()

        p_da = ps("p_da", [P, DH, T])
        p_y = ps("p_y", [P, DH, T])
        p_c = ps("p_c", [P, 2, T])
        p_m = ps("p_m", [P, 2, T])
        p_m_flat = p_m[:, :, :].rearrange("p a t -> p (a t)")
        p_m_tok = p_m[:, :, :].rearrange("p a (k d) -> p (a k) d", d=D)

        s_small_in = sem("s_small_in")
        s_w_in = sem("s_w_in")
        s_x_in = sem("s_x_in")
        s_out = sem("s_out")
        s_fill = sem("s_fill")
        s_const = sem("s_const")
        s_ones = sem("s_ones")
        s_wfloat = sem("s_wfloat")
        s_wt_ps = sem("s_wt_ps")
        s_wt = sem("s_wt")
        s_a_exp = sem("s_a_exp")
        s_neg_a = sem("s_neg_a")
        s_skip1 = sem("s_skip1")
        s_skip_diag = sem("s_skip_diag")
        s_xt_ps = sem("s_xt_ps")
        s_xt = sem("s_xt")
        s_rank_ps = sem("s_rank_ps")
        s_proj_ps = sem("s_proj_ps")
        s_part1 = sem("s_part1")
        s_rank = sem("s_rank")
        s_rest = sem("s_rest")
        s_part2 = sem("s_part2")
        s_parts = sem("s_parts")
        s_dt_ps = sem("s_dt_ps")
        s_sp_abs = sem("s_sp_abs")
        s_sp_relu = sem("s_sp_relu")
        s_sp_exp = sem("s_sp_exp")
        s_sp_log = sem("s_sp_log")
        s_dt = sem("s_dt")
        s_u = sem("s_u")
        s_rows = sem("s_rows")
        s_rows_dram = sem("s_rows_dram")
        s_b = [sem(f"s_b{k}") for k in range(N // B_GROUP)]
        s_ub = sem("s_ub")
        s_da = sem("s_da")
        s_scan = sem("s_scan")
        s_carry = sem("s_carry")
        s_c_ps = sem("s_c_ps")
        s_c = sem("s_c")
        s_hc_dve = sem("s_hc_dve")
        s_hc_pool = sem("s_hc_pool")
        s_y = sem("s_y")
        s_z = sem("s_z")
        s_zt_ps = sem("s_zt_ps")
        s_stats = [sem(f"s_stats{k}") for k in range(2)]
        s_mean = [sem(f"s_mean{k}") for k in range(2)]
        s_ln_a = [sem(f"s_ln_a{k}") for k in range(2)]
        s_ln_b = [sem(f"s_ln_b{k}") for k in range(2)]
        s_ln = [sem(f"s_ln{k}") for k in range(2)]
        s_x1 = sem("s_x1")
        s_x1t_ps = sem("s_x1t_ps")
        s_x1_hi = sem("s_x1_hi")
        s_x1_lo = sem("s_x1_lo")
        s_gate_ps = sem("s_gate_ps")
        s_up_ps = sem("s_up_ps")
        s_tanh = sem("s_tanh")
        s_silu = sem("s_silu")
        s_hid = sem("s_hid")
        s_hid_hi = sem("s_hid_hi")
        s_hid_lo = sem("s_hid_lo")
        s_o_ps = sem("s_o_ps")
        s_res = sem("s_res")
        s_out_ready = sem("s_out_ready")

        block = ctx.enter_context(nc.Block())

        def wait(eng, s, value):
            if not isinstance(value, int) or value > 0:
                eng.wait_ge(s, value)

        def units(c, s):
            return N * c + (s + 1)

        def wait_hc(eng, c, s):
            if s in POOL_STATES:
                wait(eng, s_hc_pool, NP * c + (POOL_STATES.index(s) + 1))
            else:
                wait(eng, s_hc_dve, ND * c + (sum(q not in POOL_STATES for q in range(s)) + 1))

        def unit_at(c, s, k, par):
            if s + k < 0:
                return c - 1, s + k + N, 1 - par
            if s + k >= N:
                return c + 1, s + k - N, 1 - par
            return c, s + k, par

        def sums(c, s):
            return N * c + (SUM_ORDER.index(s) + 1)

        def over_chunks(eng, step):
            step(0, 0, 0, True, True, False, False)
            step(1, 1, 0, True, True, True, False)
            with eng.Fori(0, CHUNKS // 2 - 2) as i:
                step(2 * i + 2, 0, i + 1, True, True, True, True)
                step(2 * i + 3, 1, i + 1, True, True, True, True)
            step(CHUNKS - 2, 0, CHUNKS // 2 - 1, True, True, True, True)
            step(CHUNKS - 1, 1, CHUNKS // 2 - 1, False, True, True, True)
            step(CHUNKS, 0, CHUNKS // 2, False, False, True, True)
            step(CHUNKS + 1, 1, CHUNKS // 2, False, False, False, True)

        SMALL_LOADS = 6

        @block.sync
        def _(sp):
            sp.sem_inc(s_out, 16)
            sp.dma_start(x_in[:, :, :], x_chunks[0]).then_inc(s_x_in, 16)
            sp.dma_start(w_xproj_rows[:, :], w_xproj).then_inc(s_small_in, 16)
            sp.dma_start(w_dt_rows[:, :, :], w_dt.rearrange("(h p) r -> p h r", p=P)).then_inc(s_small_in, 16)
            sp.dma_start(wt_dt[R:R + 1, :, :],
                         b_dt.rearrange("(a h p) -> a h p", a=1, p=P)).then_inc(s_small_in, 16)
            sp.dma_start(a_raw[:, :, :], a_log.rearrange("(h p) n -> p h n", p=P)).then_inc(s_small_in, 16)
            for q in range(DH):
                sp.dma_start(skip_raw[:, q:q + 1],
                             d_skip[q * P:(q + 1) * P].rearrange("(p a) -> p a", a=1)).then_inc(s_small_in, 16)
            sp.dma_start(w_int[0].rearrange("p (j d) -> p j d", d=D),
                         w_gate.rearrange("(j p) d -> p j d", p=P)).then_inc(s_w_in, 16)
            sp.dma_start(w_int[1].rearrange("p (j d) -> p j d", d=D),
                         w_up.rearrange("(j p) d -> p j d", p=P)).then_inc(s_w_in, 16)
            sp.dma_start(w_int[2].rearrange("p (q f) -> p q f", q=DH),
                         w_down.rearrange("(q p) f -> p q f", p=P)).then_inc(s_w_in, 16)
            wait(sp, s_xt_ps, 1)
            sp.dma_start(x_in[:, :, :], x_chunks[1]).then_inc(s_x_in, 16)

            def store(c):
                wait(sp, s_out_ready, c + 1)
                sp.dma_start(out_chunks[bass.ds(c, 1)].rearrange("a p k d -> (a p) k d"),
                             res_n[:, :, :]).then_inc(s_out, 16)

            def load(c):
                wait(sp, s_xt_ps, c)
                sp.dma_start(x_in[:, :, :],
                             x_chunks[bass.ds(c, 1)].rearrange("a p k d -> (a p) k d")).then_inc(s_x_in, 16)

            def broadcasts(c, par):
                wait(sp, s_rows, c + 1)
                sp.dma_start(bc_dram[par], bc_rows[:, :]).then_inc(s_rows_dram, 16)
                wait(sp, s_rows_dram, 16 * (c + 1))
                for k in range(N // B_GROUP):
                    states = slice(k * B_GROUP, (k + 1) * B_GROUP)
                    if not (isinstance(c, int) and c == 0):
                        wait(sp, s_ub, units(c - 1, states.stop - 1))
                    sp.dma_start(b_bc[:, states, :],
                                 bc_dram[par:par + 1, states, :].broadcast_to([P, B_GROUP, T])).then_inc(s_b[k], 16)
                wait(sp, s_hc_pool, NP * c)
                for run in POOL_RUNS:
                    i = POOL_STATES.index(run[0])
                    sp.dma_start(c_bc[:, i:i + len(run), :],
                                 bc_dram[par:par + 1, N + run[0]:N + run[-1] + 1, :].broadcast_to(
                                     [P, len(run), T])).then_inc(s_c, 16)

            broadcasts(0, 0)

            def step(c, par, batch, nxt, core, prev, last):
                if nxt and not (isinstance(c, int) and c + 2 >= CHUNKS):
                    load(c + 2)
                if last:
                    store(c - 2)
                if nxt:
                    broadcasts(c + 1, 1 - par)
            over_chunks(sp, step)
            sp.wait_ge(s_out, 16 * (CHUNKS + 1))

        @block.gpsimd
        def _(pool):
            nc.gpsimd.memset(ident[:, :], 0.0).then_inc(s_fill, 1)
            nc.gpsimd.memset(selector[:, :, :], 0.0).then_inc(s_fill, 1)
            nc.gpsimd.memset(eps_tile[:, :], EPS)
            nc.gpsimd.memset(neg_half[:, :], -0.5)
            nc.gpsimd.memset(neg_one[:, :], -1.0)
            pool.wait_ge(s_fill, 2)
            nc.gpsimd.affine_select(out=ident[:, :], in_=ident[:, :], compare_op=ALU.not_equal, fill=1.0,
                                    base=0, pattern=[[-1, P]], channel_multiplier=1).then_inc(s_const, 1)
            for part in range(3):
                pool.wait_ge(s_const, part + 1)
                nc.gpsimd.affine_select(out=selector[:, :, :], in_=selector[:, :, :], compare_op=ALU.not_equal,
                                        fill=1.0, base=-(BC * part + N), pattern=[[-1, N], [0, P]],
                                        channel_multiplier=1).then_inc(s_const, 1)

            def third_part(c, par):
                wait(pool, s_part2, 2 * (c + 1))
                nc.gpsimd.tensor_tensor(bc_parts[0:BC, par, :], bc_rest[0:BC, :], bc_mid[:, :],
                                        ALU.subtract).then_inc(s_parts, 1)

            def u_of(c, par):
                wait(pool, s_dt, c + 1)
                nc.gpsimd.tensor_tensor(u[:, par, :, :], dt[:, par, :, :], x_t[:, par, :, :],
                                        ALU.mult).then_inc(s_u, 1)

            def times_b(c, s, par):
                wait(pool, s_u, c + 1)
                wait(pool, s_b[s // B_GROUP], 16 * (c + 1))
                wait(pool, s_scan, 2 * (units(c, s) - UB_SLOTS))
                nc.gpsimd.tensor_tensor(ub[:, s % UB_SLOTS, :, :], u[:, par, :, :],
                                        b_bc[:, s:s + 1, :].broadcast_to([P, DH, T]),
                                        ALU.mult).then_inc(s_ub, 1)

            def times_c(c, s, par, batch):
                i = POOL_STATES.index(s)
                wait(pool, s_c, 16 * len(POOL_RUNS) * (c + 1))
                wait(pool, s_scan, 2 * units(c, s))
                if par == 0:
                    wait(pool, s_carry, units(batch, s))
                nc.gpsimd.tensor_tensor(h[:, s % H_SLOTS, :, :], h[:, s % H_SLOTS, :, :],
                                        c_bc[:, i:i + 1, :].broadcast_to([P, DH, T]),
                                        ALU.mult).then_inc(s_hc_pool, 1)

            def norm_scalars(k, count):
                wait(pool, s_mean[k], count)
                nc.gpsimd.tensor_tensor(var_eps[:, k, :], mean_var[:, k, :, 1], eps_tile[:, :],
                                        ALU.add).then_inc(s_ln_a[k], 1)
                nc.gpsimd.tensor_tensor(neg_mean[:, k, :], mean_var[:, k, :, 0], neg_one[:, :],
                                        ALU.mult).then_inc(s_ln_a[k], 1)
                wait(pool, s_ln_a[k], 2 * count)
                nc.gpsimd.tensor_tensor(rstd[:, k, :], var_eps[:, k, :], neg_half[:, :],
                                        ALU.pow).then_inc(s_ln_b[k], 1)
                wait(pool, s_ln_b[k], count)
                nc.gpsimd.tensor_tensor(shift[:, k, :], neg_mean[:, k, :], rstd[:, k, :],
                                        ALU.mult).then_inc(s_ln[k], 1)

            def low_half(c, j):
                wait(pool, s_hid_hi, NH * c + (j + 1))
                nc.gpsimd.tensor_tensor(hid16[:, 1, j, :], hid[:, j % 2, :], hid16[:, 0, j, :],
                                        ALU.subtract).then_inc(s_hid_lo, 1)

            third_part(0, 0)
            u_of(0, 0)
            for s in range(UB_AHEAD):
                times_b(0, s, 0)

            def step(c, par, batch, nxt, core, prev, last):
                for s in range(N):
                    if last and s + N - 11 in range(NH):
                        low_half(c - 2, s + N - 11)
                    if last and s == 4:
                        norm_scalars(1, c - 1)
                    if prev and s == 7:
                        norm_scalars(0, c)
                    if core:
                        ca, sa, pa = unit_at(c, s, UB_AHEAD, par)
                        if sa >= UB_AHEAD or nxt:
                            times_b(ca, sa, pa)
                    if nxt and s == 8:
                        third_part(c + 1, 1 - par)
                    if nxt and s == 12:
                        u_of(c + 1, 1 - par)
                    if core and s - POOL_LAG in POOL_STATES:
                        times_c(c, s - POOL_LAG, par, batch)
                    if prev and s - 11 in range(NH):
                        low_half(c - 1, s - 11)
            over_chunks(pool, step)

        @block.scalar
        def _(act):
            act.wait_ge(s_small_in, 16 * SMALL_LOADS)
            nc.scalar.activation(neg_a[:, :, :], a_raw[:, :, :], ACT.Exp).then_inc(s_a_exp, 1)
            act.wait_ge(s_wt_ps, 1)
            nc.scalar.copy(wt_rank[:, :, :], p_m[:, 0, 0:DH * (R + BC)].rearrange(
                "p (q r) -> p q r", q=DH)[:, :, 0:R]).then_inc(s_wt, 1)
            for part in range(3):
                nc.scalar.copy(wt_bc[:, :, part * BC:(part + 1) * BC],
                               p_m[:, 0, 0:DH * (R + BC)].rearrange(
                                   "p (q r) -> p q r", q=DH)[:, :, R:R + BC]).then_inc(s_wt, 1)
            nc.scalar.copy(wt_dt[0:R, :, :], p_m[0:R, 1, 0:DH * P].rearrange(
                "p (q r) -> p q r", q=DH)).then_inc(s_wt, 1)
            act.wait_ge(s_neg_a, 1)
            act.wait_ge(s_skip1, 1)
            act.wait_ge(s_const, 1)
            for q in range(DH):
                nc.scalar.mul(skip_diag[:, q, :], ident[:, :], skip1[:, q:q + 1]).then_inc(s_skip_diag, 1)
            dsts = ([wt_gate[:, q, :] for q in range(DH)] + [wt_up[:, q, :] for q in range(DH)]
                    + [wt_down[:, 3 * q:3 * q + 3, :].rearrange("p j d -> p (j d)") for q in range(2)])
            for n, dst in enumerate(dsts):
                act.wait_ge(s_wt_ps, n + 2)
                nc.scalar.copy(dst, p_m_flat[:, 0:HID]).then_inc(s_wt, 1)

            def x_out(c, par):
                wait(act, s_xt_ps, c + 1)
                nc.scalar.copy(x_t[:, par, :, :], p_m[:, :, :]).then_inc(s_xt, 1)

            def rank_out(c):
                wait(act, s_rank_ps, c + 1)
                nc.scalar.copy(rank_t[0:R, :], p_m[0:R, 1, :]).then_inc(s_rank, 1)

            def bc_out(c, par):
                wait(act, s_proj_ps, c + 1)
                wait(act, s_rows_dram, 16 * c)
                nc.scalar.copy(bc_rows[:, :], p_m[0:BC, 0, :]).then_inc(s_rows, 1)
                nc.scalar.copy(bc_parts[:, par, :], p_m[0:3 * BC, 0, :]).then_inc(s_part1, 1)

            def second_parts(c, par):
                wait(act, s_rest, c + 1)
                nc.scalar.copy(bc_parts[BC:2 * BC, par, :], bc_rest[BC:2 * BC, :]).then_inc(s_part2, 1)
                nc.scalar.copy(bc_mid[:, :], bc_rest[0:BC, :]).then_inc(s_part2, 1)

            def softplus_in(c):
                wait(act, s_dt_ps, c + 1)
                nc.scalar.activation(sp_abs[:, :, :], p_m[:, :, :], ACT.Abs).then_inc(s_sp_abs, 1)
                nc.scalar.activation(sp_relu[:, :, :], p_m[:, :, :], ACT.Relu).then_inc(s_sp_relu, 1)

            def softplus_exp(c):
                wait(act, s_sp_abs, c + 1)
                nc.scalar.activation(sp_abs[:, :, :], sp_abs[:, :, :], ACT.Exp, scale=-1.0).then_inc(s_sp_exp, 1)

            def softplus_log(c):
                wait(act, s_sp_exp, c + 1)
                nc.scalar.activation(sp_abs[:, :, :], sp_abs[:, :, :], ACT.Ln, bias=1.0).then_inc(s_sp_log, 1)

            def decay(c, s, par, q):
                wait(act, s_dt, c + 1)
                wait(act, s_scan, 2 * units(c, s) - 2 + q - 1)
                nc.scalar.activation(p_da[:, q, :], dt[:, par, q, :], ACT.Exp,
                                     scale=neg_a[:, q, s:s + 1]).then_inc(s_da, 1)

            def z_out(c):
                wait(act, s_y, N * (c + 1))
                nc.scalar.copy(z[:, :, :], p_y[:, :, :]).then_inc(s_z, 1)

            def norm1(c):
                wait(act, s_zt_ps, c + 1)
                wait(act, s_ln[0], c + 1)
                for k in range(TT):
                    nc.scalar.activation(x1[:, k, :], p_m_tok[:, k, :], ACT.Identity, bias=shift[:, 0, k:k + 1],
                                         scale=rstd[:, 0, k:k + 1]).then_inc(s_x1, 1)

            def x1_high(c):
                wait(act, s_x1t_ps, c + 1)
                nc.scalar.mul(x1_t[:, 0, :, :], p_m[:, :, :], X1_SCALE).then_inc(s_x1_hi, 1)

            def tanh_of(c, j):
                wait(act, s_gate_ps, NH * c + (j + 1))
                nc.scalar.activation(tanh_g[:, :], p_m[:, 0, :], ACT.Tanh,
                                     scale=0.5 / (QUANT * X1_SCALE)).then_inc(s_tanh, 1)

            def high_half(c, j):
                wait(act, s_hid, NH * c + (j + 1))
                nc.scalar.copy(hid16[:, 0, j, :], hid[:, j % 2, :]).then_inc(s_hid_hi, 1)

            def norm2(c):
                wait(act, s_ln[1], c + 1)
                wait(act, s_res, 2 * (c + 1))
                wait(act, s_out, 16 * (c + 1))
                for k in range(TT):
                    ins = nc.scalar.activation(res_n[:, k, :], res[:, k, :], ACT.Identity,
                                               bias=shift[:, 1, k:k + 1], scale=rstd[:, 1, k:k + 1])
                ins.then_inc(s_out_ready, 1)

            x_out(0, 0)
            rank_out(0)
            bc_out(0, 0)
            second_parts(0, 0)
            softplus_in(0)
            softplus_exp(0)
            softplus_log(0)
            for q in range(DH):
                decay(0, 0, 0, q)

            def step(c, par, batch, nxt, core, prev, last):
                for s in range(N):
                    if prev and s == 2:
                        z_out(c - 1)
                    if nxt and s == 4:
                        rank_out(c + 1)
                    if prev and s == 8:
                        x1_high(c - 1)
                    if nxt and s == 9:
                        softplus_in(c + 1)
                    if last and s + N - 11 in range(NH):
                        high_half(c - 2, s + N - 11)
                    if prev and s - 11 in range(NH):
                        high_half(c - 1, s - 11)
                    if prev and s - 10 in range(NH):
                        tanh_of(c - 1, s - 10)
                    if core:
                        ce, se, pe_ = unit_at(c, s, DA_AHEAD, par)
                        if se >= DA_AHEAD or nxt:
                            for q in range(DH):
                                decay(ce, se, pe_, q)
                    if nxt and s == 3:
                        x_out(c + 1, 1 - par)
                    if nxt and s == 4:
                        bc_out(c + 1, 1 - par)
                    if nxt and s == 6:
                        second_parts(c + 1, 1 - par)
                    if last and s == 5:
                        norm2(c - 2)
                    if prev and s == 7:
                        norm1(c - 1)
                    if nxt and s == 10:
                        softplus_exp(c + 1)
                    if nxt and s == 11:
                        softplus_log(c + 1)
            over_chunks(act, step)

        @block.vector
        def _(dve):
            nc.vector.memset(rank_t[R:R + 1, :], 1.0).then_inc(s_ones, 1)
            dve.wait_ge(s_a_exp, 1)
            nc.vector.tensor_scalar_mul(neg_a[:, :, :], neg_a[:, :, :], -1.0).then_inc(s_neg_a, 1)
            nc.vector.tensor_scalar_add(skip1[:, :], skip_raw[:, :], 1.0).then_inc(s_skip1, 1)
            dve.wait_ge(s_w_in, 16 * 3)
            for n in range(3):
                nc.vector.tensor_copy(w_float[n], w_int[n]).then_inc(s_wfloat, 1)

            def rest(c, par):
                wait(dve, s_proj_ps, c + 1)
                wait(dve, s_part1, c + 1)
                nc.vector.tensor_tensor(bc_rest[:, :], p_m[0:3 * BC, 0, :], bc_parts[:, par, :],
                                        ALU.subtract).then_inc(s_rest, 1)

            def dt_of(c, par):
                wait(dve, s_sp_relu, c + 1)
                wait(dve, s_sp_log, c + 1)
                nc.vector.tensor_tensor(dt[:, par, :, :], sp_relu[:, :, :], sp_abs[:, :, :],
                                        ALU.add).then_inc(s_dt, 1)

            def scan(c, s, par, batch, q):
                wait(dve, s_da, 2 * units(c, s) - 1 + q)
                if q == 0:
                    wait(dve, s_ub, units(c, s))
                    ch, sh, _ = unit_at(c, s, -H_SLOTS, par)
                    if not (isinstance(ch, int) and ch < 0):
                        wait(dve, s_y, sums(ch, sh))
                if par == 0:
                    initial = 0.0
                else:
                    initial = h_carry[:, s, q:q + 1]
                    if q == 0:
                        wait(dve, s_carry, units(batch, s))
                nc.vector.tensor_tensor_scan(h[:, s % H_SLOTS, q, :], p_da[:, q, :], ub[:, s % UB_SLOTS, q, :],
                                             initial, ALU.mult, ALU.add).then_inc(s_scan, 1)

            def carry(c, s):
                wait(dve, s_scan, 2 * units(c, s))
                nc.vector.tensor_copy(h_carry[:, s, :], h[:, s % H_SLOTS, :, T - 1]).then_inc(s_carry, 1)

            def times_c(c, s, par, batch):
                i = DVE_STATES.index(s)
                wait(dve, s_c_ps, ND * c + (i + 1))
                wait(dve, s_scan, 2 * units(c, s))
                if par == 0:
                    wait(dve, s_carry, units(batch, s))
                nc.vector.tensor_tensor(h[:, s % H_SLOTS, :, :], h[:, s % H_SLOTS, :, :],
                                        p_c[:, i % 2:i % 2 + 1, :].broadcast_to([P, DH, T]),
                                        ALU.mult).then_inc(s_hc_dve, 1)

            def norm_stats(k, src):
                for t in range(TT):
                    nc.vector.bn_stats(stats[:, k, t, :], src[:, t, :]).then_inc(s_stats[k], 1)

            def norm_mean(k):
                for t in range(TT):
                    ins = nc.vector.bn_aggr(mean_var[:, k, t, :], stats[:, k, t, :])
                ins.then_inc(s_mean[k], 1)

            def x1_low(c):
                wait(dve, s_x1_hi, c + 1)
                nc.vector.scalar_tensor_tensor(x1_t[:, 1, :, :], p_m[:, :, :], X1_SCALE, x1_t[:, 0, :, :],
                                               ALU.mult, ALU.subtract).then_inc(s_x1_lo, 1)

            def silu_of(c, j):
                wait(dve, s_tanh, NH * c + (j + 1))
                nc.vector.scalar_tensor_tensor(silu_g[:, :], tanh_g[:, :], 1.0, p_m[:, 0, :],
                                               ALU.add, ALU.mult).then_inc(s_silu, 1)

            def hidden(c, j):
                wait(dve, s_up_ps, NH * c + (j + 1))
                wait(dve, s_silu, NH * c + (j + 1))
                if j >= 2:
                    wait(dve, s_hid_lo, NH * c + (j - 1))
                nc.vector.scalar_tensor_tensor(hid[:, j % 2, :], p_m[:, 1, :],
                                               H_SCALE / (2.0 * QUANT * QUANT * X1_SCALE * X1_SCALE),
                                               silu_g[:, :], ALU.mult, ALU.mult).then_inc(s_hid, 1)

            def residual(c, a):
                wait(dve, s_o_ps, 2 * c + (a + 1))
                nc.vector.scalar_tensor_tensor(
                    res[:, 2 * a:2 * a + 2, :], p_m_tok[:, 2 * a:2 * a + 2, :], 1.0 / (QUANT * H_SCALE),
                    x1[:, 2 * a:2 * a + 2, :], ALU.mult, ALU.add).then_inc(s_res, 1)

            rest(0, 0)
            dt_of(0, 0)

            def step(c, par, batch, nxt, core, prev, last):
                for s in range(N):
                    if last and s == 2:
                        residual(c - 2, 0)
                    if nxt and s == 5:
                        rest(c + 1, 1 - par)
                    if prev and s == 6:
                        wait(dve, s_zt_ps, c)
                        norm_stats(0, p_m_tok)
                    if nxt and s == 12:
                        dt_of(c + 1, 1 - par)
                    if core:
                        scan(c, s, par, batch, 0)
                    cb, sb_, pb = unit_at(c, s, -1, par)
                    last_unit = core and s > 0 or prev and s == 0
                    if last_unit and pb == 0:
                        carry(cb, sb_)
                    if last and s == 3:
                        wait(dve, s_res, 2 * (c - 1))
                        norm_stats(1, res)
                        wait(dve, s_stats[1], TT * (c - 1))
                    if prev and s == 6:
                        wait(dve, s_stats[0], TT * c)
                    if core:
                        scan(c, s, par, batch, 1)
                    if last and s == 3:
                        norm_mean(1)
                    if prev and s == 6:
                        norm_mean(0)
                    if prev and s == 8:
                        x1_low(c - 1)
                    if prev and s - 10 in range(NH):
                        silu_of(c - 1, s - 10)
                    if last_unit and sb_ not in POOL_STATES:
                        times_c(cb, sb_, pb, batch)
                    if prev and s - 10 in range(NH):
                        hidden(c - 1, s - 10)
                    if last and s == 2:
                        residual(c - 2, 1)
            over_chunks(dve, step)

        @block.tensor
        def _(pe):
            pe.wait_ge(s_const, 4)
            pe.wait_ge(s_small_in, 16 * SMALL_LOADS)
            for q in range(DH):
                nc.tensor.transpose(p_m[:, 0, q * (R + BC):(q + 1) * (R + BC)],
                                    w_xproj_rows[:, q * P:(q + 1) * P], ident[0:R + BC, 0:R + BC])
            for q in range(DH):
                ins = nc.tensor.transpose(p_m[0:R, 1, q * P:(q + 1) * P], w_dt_rows[:, q, :], ident[:, :])
            ins.then_inc(s_wt_ps, 1)
            pe.wait_ge(s_wt, 5)
            w_tiles = [w_float[n].rearrange("p (j d) -> p j d", d=D) for n in range(2)]
            w_down_tiles = w_float[2].rearrange("p (q f) -> p q f", q=DH)
            pe.wait_ge(s_wfloat, 3)
            for n in range(4):
                if n:
                    pe.wait_ge(s_wt, 5 + n)
                for j in range(NH):
                    ins = nc.tensor.transpose(p_m_flat[:, j * P:(j + 1) * P],
                                              w_tiles[n // DH][:, j, (n % DH) * P:(n % DH + 1) * P], ident[:, :])
                ins.then_inc(s_wt_ps, 1)
            for n in range(2):
                pe.wait_ge(s_wt, 9 + n)
                for j in range(3):
                    for q in range(DH):
                        ins = nc.tensor.transpose(
                            p_m_flat[:, (DH * j + q) * P:(DH * j + q + 1) * P],
                            w_down_tiles[:, q, (3 * n + j) * P:(3 * n + j + 1) * P], ident[:, :])
                ins.then_inc(s_wt_ps, 1)
            pe.wait_ge(s_wt, 11)

            def x_transposed(c):
                wait(pe, s_x_in, 16 * (c + 1))
                if isinstance(c, int) and c <= 2:
                    wait(pe, s_sp_relu, c)
                else:
                    wait(pe, s_res, 2 * (c - 2))
                for q in range(DH):
                    for k in range(TT):
                        ins = nc.tensor.transpose(p_m[:, q, k * P:(k + 1) * P],
                                                  x_in[:, k, q * P:(q + 1) * P], ident[:, :])
                ins.then_inc(s_xt_ps, 1)

            def project_rank(c, par):
                wait(pe, s_xt, c + 1)
                for q in range(DH):
                    ins = nc.tensor.matmul(p_m[0:R, 1, :], wt_rank[:, q, :], x_t[:, par, q, :],
                                           start=(q == 0), stop=(q == DH - 1))
                ins.then_inc(s_rank_ps, 1)

            def project_bc(c, par):
                for q in range(DH):
                    ins = nc.tensor.matmul(p_m[0:3 * BC, 0, :], wt_bc[:, q, :], x_t[:, par, q, :],
                                           start=(q == 0), stop=(q == DH - 1))
                ins.then_inc(s_proj_ps, 1)

            def project_dt(c):
                wait(pe, s_rank, c + 1)
                wait(pe, s_rest, c + 1)
                for q in range(DH):
                    ins = nc.tensor.matmul(p_m[:, q, :], wt_dt[:, q, :], rank_t[:, :], start=True, stop=True)
                ins.then_inc(s_dt_ps, 1)

            def broadcast_c(c, s, par):
                i = DVE_STATES.index(s)
                wait(pe, s_parts, c + 1)
                wait(pe, s_hc_dve, ND * c + (i - 1))
                nc.tensor.matmul(p_c[:, i % 2, :], selector[:, s, :], bc_parts[:, par, :],
                                 start=True, stop=True).then_inc(s_c_ps, 1)

            def sum_states(c, s, par):
                if s == SUM_ORDER[0]:
                    wait(pe, s_z, c)
                    for q in range(DH):
                        nc.tensor.matmul(p_y[:, q, :], skip_diag[:, q, :], x_t[:, par, q, :],
                                         start=True, stop=False)
                wait_hc(pe, c, s)
                for q in range(DH):
                    ins = nc.tensor.matmul(p_y[:, q, :], ident[:, :], h[:, s % H_SLOTS, q, :],
                                           start=False, stop=(s == SUM_ORDER[-1]))
                ins.then_inc(s_y, 1)

            def z_transposed(c):
                wait(pe, s_z, c + 1)
                for k in range(TT):
                    for q in range(DH):
                        ins = nc.tensor.transpose(p_m_tok[:, k, q * P:(q + 1) * P],
                                                  z[:, q, k * P:(k + 1) * P], ident[:, :])
                ins.then_inc(s_zt_ps, 1)

            def x1_transposed(c):
                wait(pe, s_x1, TT * (c + 1))
                for q in range(DH):
                    for k in range(TT):
                        ins = nc.tensor.transpose(p_m[:, q, k * P:(k + 1) * P],
                                                  x1[:, k, q * P:(q + 1) * P], ident[:, :])
                ins.then_inc(s_x1t_ps, 1)

            def gate_up(c, j):
                wait(pe, s_x1_lo, c + 1)
                for a, w, free, done in ((0, wt_gate, s_silu, s_gate_ps), (1, wt_up, s_hid, s_up_ps)):
                    if j:
                        wait(pe, free, NH * c + j)
                    for n in range(2 * DH):
                        ins = nc.tensor.matmul(p_m[:, a, :], w[:, n % DH, j * P:(j + 1) * P],
                                               x1_t[:, n // DH, n % DH, :],
                                               start=(n == 0), stop=(n == 2 * DH - 1))
                    ins.then_inc(done, 1)

            def down(c, a):
                wait(pe, s_hid_lo, NH * (c + 1))
                for k in (2 * a, 2 * a + 1):
                    for n in range(2 * NH):
                        ins = nc.tensor.matmul(p_m_tok[:, k, :], hid16[:, n // NH, n % NH, k * P:(k + 1) * P],
                                               wt_down[:, n % NH, :], start=(n == 0), stop=(n == 2 * NH - 1))
                ins.then_inc(s_o_ps, 1)

            x_transposed(0)
            project_rank(0, 0)
            project_bc(0, 0)
            pe.wait_ge(s_ones, 1)
            project_dt(0)

            def step(c, par, batch, nxt, core, prev, last):
                for s in range(N):
                    if core and s in DVE_STATES:
                        broadcast_c(c, s, par)
                    if last and s == 1:
                        down(c - 2, 0)
                    if nxt and s == 3:
                        x_transposed(c + 1)
                    if nxt and s == 4:
                        project_bc(c + 1, 1 - par)
                    for cy, sy, py in (unit_at(c, s, -lag, par) for lag in sorted(SUM_LAG.values(), reverse=True)):
                        here = sy + SUM_LAG[sy in POOL_STATES]
                        if here == s and core or here == s + N and prev:
                            sum_states(cy, sy, py)
                    if last and s == 1:
                        down(c - 2, 1)
                    if nxt and s == 3:
                        project_rank(c + 1, 1 - par)
                    if prev and s == 5:
                        if nxt:
                            wait(pe, s_rank, c + 2)
                            wait(pe, s_rest, c + 2)
                        elif last:
                            wait(pe, s_res, 2 * (c - 1))
                        z_transposed(c - 1)
                    if prev and s == 7:
                        x1_transposed(c - 1)
                    if nxt and s == 8:
                        if prev:
                            wait(pe, s_x1_lo, c)
                        project_dt(c + 1)
                    if prev and s - 9 in range(NH):
                        if nxt and s == 9:
                            wait(pe, s_sp_relu, c + 2)
                        gate_up(c - 1, s - 9)
            over_chunks(pe, step)


_INS = ['L0_attn_x', 'L0_attn_W_xproj', 'L0_attn_W_dt', 'L0_attn_b_dt', 'L0_attn_A_log', 'L0_attn_Dp',
        'L0_ffn_w_gate', 'L0_ffn_w_up', 'L0_ffn_w_down']


def kernel(**inputs):
    import numpy as _np
    import concourse.bacc as _bacc
    from concourse import mybir as _mybir
    from concourse.bass_utils import run_bass_kernel_spmd as _run

    nc = _bacc.Bacc("TRN2", target_bir_lowering=False, num_devices=1)
    arrays, args = {}, []
    for name in _INS:
        a = _np.ascontiguousarray(inputs[name])
        arrays[f"in_{name}"] = a
        args.append(nc.dram_tensor(f"in_{name}", a.shape, _mybir.dt.from_np(a.dtype), kind="ExternalInput").ap())
    out = nc.dram_tensor("out_x", inputs['L0_attn_x'].shape, _mybir.dt.float32, kind="ExternalOutput").ap()
    mamba_ffn_block(nc, *args, out)
    r = _run(nc, [arrays], core_ids=[0])
    return r.results[0]["out_x"]
```

```python
from contextlib import ExitStack

import concourse.bass as bass
from concourse import mybir

P = 128
F32 = mybir.dt.float32
BF16 = mybir.dt.bfloat16
F16 = mybir.dt.float16
I32 = mybir.dt.int32
ALU = mybir.AluOpType
ACT = mybir.ActivationFunctionType

T = 512
EPS = 1e-5
QUANT = 127.0
X1_SCALE = 2.0 ** 11
H_SCALE = 2.0 ** -1

POOL_STATES = (0, 3, 4, 7)

UB_AHEAD = 4
DA_AHEAD = 1
C_LAG = 1
POOL_LAG = 1
SUM_LAG = {True: 3, False: 2}

AT = {
    "weights": (7, 1),
    "x_transposed": (0, 0), "x_out": (0, 0), "project": (1, 0),
    "rank_out": (1, 0), "bc_out": (1, 1), "rest": (2, 1),
    "second_parts": (2, 1), "third_part": (9, 0),
    "project_dt": (2, 2), "softplus_in": (3, 0), "softplus_exp": (4, 0), "softplus_log": (5, 0),
    "dt_of": (6, 2), "u_of": (9, 1),
    "z_out": (2, 1), "z_transposed": (3, 1), "stats1": (5, 1), "mean1": (5, 1),
    "norm_inputs": (6, 0), "scalars": (6, 0), "norm1": (7, 0),
    "x1_transposed": (7, 2), "x1_high": (8, 0), "x1_low": (9, 0),
    "gate_up": (9, 2), "tanh": (9, 1), "silu": (10, 0), "hidden": (10, 0),
    "high_half": (10, 0), "low_half": (10, 0),
    "down0": (1, 2), "down1": (2, 2), "down2": (3, 0), "down3": (3, 1),
    "residual0": (3, 0), "residual1": (5, 0), "stats2": (5, 1), "mean2": (5, 1),
    "norm2": (9, 0),
}

B_GROUP = 4
UB_SLOTS = 8
H_SLOTS = 8


def mamba_ffn_block(nc, x, w_xproj, w_dt, b_dt, a_log, d_skip, w_gate, w_up, w_down, out):
    BATCH, SEQ, D = x.shape
    N = a_log.shape[1]
    R = w_dt.shape[1]
    HID = w_gate.shape[0]
    DH = D // P
    NH = HID // P
    TT = T // P
    CHUNKS = BATCH * SEQ // T
    BC = 2 * N
    assert DH == 2 and SEQ == 2 * T and CHUNKS >= 4 and N == 16 and NH == 6 and R == 64 and R + 2 * BC == P
    NP = len(POOL_STATES)
    ND = N - NP
    DVE_STATES = [s for s in range(N) if s not in POOL_STATES]
    POOL_RUNS = []
    for s in POOL_STATES:
        if POOL_RUNS and POOL_RUNS[-1][-1] == s - 1:
            POOL_RUNS[-1].append(s)
        else:
            POOL_RUNS.append([s])
    assert N % B_GROUP == N % UB_SLOTS == N % H_SLOTS == 0
    sum_at = {s: s + SUM_LAG[s in POOL_STATES] for s in range(N)}
    SUM_ORDER = sorted(range(N), key=lambda s: (sum_at[s], s))
    assert all(sum_at[s] < N or s not in POOL_STATES for s in range(N))

    x_chunks = x.rearrange("b (h k p) d -> (b h) p k d", p=P, k=TT)
    out_chunks = out.rearrange("b (h k p) d -> (b h) p k d", p=P, k=TT)

    with ExitStack() as ctx:
        def sb(name, shape, dt):
            return ctx.enter_context(nc.sbuf_tensor(name, shape, dt))

        def ps(name, shape):
            return ctx.enter_context(nc.psum_tensor(name, shape, F32))

        def sem(name):
            return ctx.enter_context(nc.semaphore(name))

        ident = sb("ident", [P, P], F32)
        selector = sb("selector", [P, N, P], BF16)
        neg_a = sb("neg_a", [P, DH, N], F32)
        a_raw = sb("a_raw", [P, DH, N], F32)
        skip_raw = sb("skip_raw", [P, DH], F32)
        skip1 = sb("skip1", [P, DH], F32)
        skip_diag = sb("skip_diag", [P, DH, P], F32)
        w_xproj_rows = sb("w_xproj_rows", [R + BC, D], F32)
        w_dt_rows = sb("w_dt_rows", [P, DH, R], F32)
        wt_proj = sb("wt_proj", [P, DH, P], F32)
        wt_dt = sb("wt_dt", [R + 1, DH, P], F32)
        wt_gate = sb("wt_gate", [P, DH, HID], F16)
        wt_up = sb("wt_up", [P, DH, HID], F16)
        wt_down = sb("wt_down", [P, NH, D], F16)
        neg_half = sb("neg_half", [P, 2, TT], F32)
        x_in = sb("x_in", [P, TT, D], F32)
        x_t = sb("x_t", [P, 2, DH, T], F32)
        rank_t = sb("rank_t", [R + 1, T], F32)
        FIRST, SECOND, THIRD = slice(R, R + BC), slice(R + BC, P), slice(0, BC)
        BOTH = slice(R, P)
        bc_rows = sb("bc_rows", [P, T], F32)
        bc_parts = sb("bc_parts", [P, 2, T], BF16)
        bc_rest = sb("bc_rest", [P, T], F32)
        bc_mid = sb("bc_mid", [P, T], BF16)
        sp_abs = sb("sp_abs", [P, DH, T], F32)
        dt = sb("dt", [P, 2, DH, T], F32)
        u = sb("u", [P, 2, DH, T], F32)
        b_bc = sb("b_bc", [P, N, T], F32)
        c_bc = sb("c_bc", [P, NP, T], F32)
        ub = sb("ub", [P, UB_SLOTS, DH, T], F32)
        h = sb("h", [P, H_SLOTS, DH, T], F32)
        h_carry = sb("h_carry", [P, N, DH], F32)
        z = sb("z", [P, DH, T], F32)
        x1 = sb("x1", [P, TT, D], F32)
        x1_t = sb("x1_t", [P, 2, DH, T], F16)
        tanh_g = sb("tanh_g", [P, T], F32)
        silu_g = sb("silu_g", [P, T], F32)
        hid = sb("hid", [P, 2, T], F32)
        hid16 = sb("hid16", [P, 2, NH, T], F16)
        res = sb("res", [P, TT, D], F32)
        res_n = sb("res_n", [P, TT, D], F32)
        w_rows = [hid16[:, n, :, :].rearrange("p j t -> p (j t)").bitcast(F32) for n in range(2)]
        w_rows += [buffer[:, :, :].rearrange("p k d -> p (k d)")[:, 0:HID] for buffer in (res, res_n)]
        stats = sb("stats", [P, 2, TT, 6], F32)
        mean_var = sb("mean_var", [P, 2, TT, 2], F32)
        var_eps = sb("var_eps", [P, 2, TT], F32)
        rstd = sb("rstd", [P, 2, TT], F32)
        neg_mean = sb("neg_mean", [P, 2, TT], F32)
        shift = sb("shift", [P, 2, TT], F32)

        bc_dram = nc.dram_tensor("bc_rows_dram", (2, BC, T), F32, kind="Internal").ap()

        p_da = ps("p_da", [P, DH, T])
        p_y = ps("p_y", [P, DH, T])
        p_c = ps("p_c", [P, 1, T])
        p_o = ps("p_o", [P, 2, D])
        p_m = ps("p_m", [P, 2, T])
        p_m_flat = p_m[:, :, :].rearrange("p a t -> p (a t)")
        p_m_tok = p_m[:, :, :].rearrange("p a (k d) -> p (a k) d", d=D)

        s_small_in = sem("s_small_in")
        s_w_in = sem("s_w_in")
        s_x_in = sem("s_x_in")
        s_out = sem("s_out")
        s_fill = sem("s_fill")
        s_const = sem("s_const")
        s_ones = sem("s_ones")
        s_wfloat = sem("s_wfloat")
        s_wt_ps = sem("s_wt_ps")
        s_wt = sem("s_wt")
        s_a_exp = sem("s_a_exp")
        s_neg_a = sem("s_neg_a")
        s_skip1 = sem("s_skip1")
        s_skip_diag = sem("s_skip_diag")
        s_xt_ps = sem("s_xt_ps")
        s_xt = sem("s_xt")
        s_proj_ps = sem("s_proj_ps")
        s_part1 = sem("s_part1")
        s_rank = sem("s_rank")
        s_rest = sem("s_rest")
        s_part2 = sem("s_part2")
        s_parts = sem("s_parts")
        s_dt_ps = sem("s_dt_ps")
        s_sp_abs = sem("s_sp_abs")
        s_sp_relu = sem("s_sp_relu")
        s_sp_exp = sem("s_sp_exp")
        s_sp_log = sem("s_sp_log")
        s_dt = sem("s_dt")
        s_u = sem("s_u")
        s_rows = sem("s_rows")
        s_rows_dram = sem("s_rows_dram")
        s_b = [sem(f"s_b{k}") for k in range(N // B_GROUP)]
        s_ub = sem("s_ub")
        s_da = sem("s_da")
        s_scan = sem("s_scan")
        s_carry = sem("s_carry")
        s_c_ps = sem("s_c_ps")
        s_c = sem("s_c")
        s_hc_dve = sem("s_hc_dve")
        s_hc_pool = sem("s_hc_pool")
        s_y = sem("s_y")
        s_z = sem("s_z")
        s_zt_ps = sem("s_zt_ps")
        s_stats = [sem(f"s_stats{k}") for k in range(2)]
        s_mean = [sem(f"s_mean{k}") for k in range(2)]
        s_ln_in = sem("s_ln_in")
        s_rstd = sem("s_rstd")
        s_ln = sem("s_ln")
        s_x1 = sem("s_x1")
        s_x1t_ps = sem("s_x1t_ps")
        s_x1_hi = sem("s_x1_hi")
        s_x1_lo = sem("s_x1_lo")
        s_gate_ps = sem("s_gate_ps")
        s_up_ps = sem("s_up_ps")
        s_tanh = sem("s_tanh")
        s_silu = sem("s_silu")
        s_hid = sem("s_hid")
        s_hid_hi = sem("s_hid_hi")
        s_hid_lo = sem("s_hid_lo")
        s_o_ps = sem("s_o_ps")
        s_res = sem("s_res")
        s_out_ready = sem("s_out_ready")

        block = ctx.enter_context(nc.Block())

        def wait(eng, s, value):
            if not isinstance(value, int) or value > 0:
                eng.wait_ge(s, value)

        def units(c, s):
            return N * c + (s + 1)

        def wait_hc(eng, c, s):
            if s in POOL_STATES:
                wait(eng, s_hc_pool, NP * c + (POOL_STATES.index(s) + 1))
            else:
                wait(eng, s_hc_dve, ND * c + (sum(q not in POOL_STATES for q in range(s)) + 1))

        def unit_at(c, s, k, par):
            if s + k < 0:
                return c - 1, s + k + N, 1 - par
            if s + k >= N:
                return c + 1, s + k - N, 1 - par
            return c, s + k, par

        def sums(c, s):
            return N * c + (SUM_ORDER.index(s) + 1)

        def over_chunks(eng, step):
            step(0, 0, 0, True, True, False, False)
            step(1, 1, 0, True, True, True, False)
            with eng.Fori(0, CHUNKS // 2 - 2) as i:
                step(2 * i + 2, 0, i + 1, True, True, True, True)
                step(2 * i + 3, 1, i + 1, True, True, True, True)
            step(CHUNKS - 2, 0, CHUNKS // 2 - 1, True, True, True, True)
            step(CHUNKS - 1, 1, CHUNKS // 2 - 1, False, True, True, True)
            step(CHUNKS, 0, CHUNKS // 2, False, False, True, True)
            step(CHUNKS + 1, 1, CHUNKS // 2, False, False, False, True)

        def due_at(s, zone):
            return lambda job: AT[job] == (s, zone)

        def tiles(job, s, zone, c, prev, last):
            for j in range(NH):
                slot = AT[job][0] + j
                if AT[job][1] == zone:
                    if slot == s and prev:
                        yield c - 1, j
                    elif slot == s + N and last:
                        yield c - 2, j

        SMALL_LOADS = 6
        WEIGHT_BATCHES = 2 * DH + 2

        @block.sync
        def _(sp):
            sp.sem_inc(s_out, 16)
            sp.dma_start(x_in[:, :, :], x_chunks[0]).then_inc(s_x_in, 16)
            sp.dma_start(w_xproj_rows[:, :], w_xproj).then_inc(s_small_in, 16)
            sp.dma_start(w_dt_rows[:, :, :], w_dt.rearrange("(h p) r -> p h r", p=P)).then_inc(s_small_in, 16)
            sp.dma_start(wt_dt[R:R + 1, :, :],
                         b_dt.rearrange("(a h p) -> a h p", a=1, p=P)).then_inc(s_small_in, 16)
            sp.dma_start(a_raw[:, :, :], a_log.rearrange("(h p) n -> p h n", p=P)).then_inc(s_small_in, 16)
            for q in range(DH):
                sp.dma_start(skip_raw[:, q:q + 1],
                             d_skip[q * P:(q + 1) * P].rearrange("(p a) -> p a", a=1)).then_inc(s_small_in, 16)
            for w, rows in ((w_gate, w_rows[0]), (w_up, w_rows[1])):
                sp.dma_start(rows.bitcast(I32).rearrange("p (j d) -> p j d", d=D),
                             w.rearrange("(j p) d -> p j d", p=P)).then_inc(s_w_in, 16)
            for q in range(DH):
                sp.dma_start(w_rows[2 + q].bitcast(I32), w_down[q * P:(q + 1) * P, :]).then_inc(s_w_in, 16)
            wait(sp, s_xt_ps, 1)
            sp.dma_start(x_in[:, :, :], x_chunks[1]).then_inc(s_x_in, 16)

            def store(c):
                wait(sp, s_out_ready, c + 1)
                sp.dma_start(out_chunks[bass.ds(c, 1)].rearrange("a p k d -> (a p) k d"),
                             res_n[:, :, :]).then_inc(s_out, 16)

            def load(c):
                wait(sp, s_xt_ps, c)
                sp.dma_start(x_in[:, :, :],
                             x_chunks[bass.ds(c, 1)].rearrange("a p k d -> (a p) k d")).then_inc(s_x_in, 16)

            def broadcasts(c, par):
                wait(sp, s_rows, c + 1)
                sp.dma_start(bc_dram[par], bc_rows[FIRST, :]).then_inc(s_rows_dram, 16)
                wait(sp, s_rows_dram, 16 * (c + 1))
                for k in range(N // B_GROUP):
                    states = slice(k * B_GROUP, (k + 1) * B_GROUP)
                    if not (isinstance(c, int) and c == 0):
                        wait(sp, s_ub, units(c - 1, states.stop - 1))
                    sp.dma_start(b_bc[:, states, :],
                                 bc_dram[par:par + 1, states, :].broadcast_to([P, B_GROUP, T])).then_inc(s_b[k], 16)
                wait(sp, s_hc_pool, NP * c)
                for run in POOL_RUNS:
                    i = POOL_STATES.index(run[0])
                    sp.dma_start(c_bc[:, i:i + len(run), :],
                                 bc_dram[par:par + 1, N + run[0]:N + run[-1] + 1, :].broadcast_to(
                                     [P, len(run), T])).then_inc(s_c, 16)

            broadcasts(0, 0)

            def step(c, par, batch, nxt, core, prev, last):
                if nxt and not (isinstance(c, int) and c + 2 >= CHUNKS):
                    load(c + 2)
                if last:
                    store(c - 2)
                if nxt:
                    broadcasts(c + 1, 1 - par)
            over_chunks(sp, step)
            sp.wait_ge(s_out, 16 * (CHUNKS + 1))

        @block.gpsimd
        def _(pool):
            nc.gpsimd.memset(ident[:, :], 0.0).then_inc(s_fill, 1)
            nc.gpsimd.memset(selector[:, :, :], 0.0).then_inc(s_fill, 1)
            nc.gpsimd.memset(neg_half[:, :, :], -0.5)
            pool.wait_ge(s_fill, 2)
            nc.gpsimd.affine_select(out=ident[:, :], in_=ident[:, :], compare_op=ALU.not_equal, fill=1.0,
                                    base=0, pattern=[[-1, P]], channel_multiplier=1).then_inc(s_const, 1)
            for part, rows in enumerate((FIRST, SECOND, THIRD)):
                pool.wait_ge(s_const, part + 1)
                nc.gpsimd.affine_select(out=selector[:, :, :], in_=selector[:, :, :], compare_op=ALU.not_equal,
                                        fill=1.0, base=-(rows.start + N), pattern=[[-1, N], [0, P]],
                                        channel_multiplier=1).then_inc(s_const, 1)

            def u_of(c, par):
                wait(pool, s_dt, c + 1)
                nc.gpsimd.tensor_tensor(u[:, par, :, :], dt[:, par, :, :], x_t[:, par, :, :],
                                        ALU.mult).then_inc(s_u, 1)

            def times_b(c, s, par):
                wait(pool, s_u, c + 1)
                wait(pool, s_b[s // B_GROUP], 16 * (c + 1))
                wait(pool, s_scan, 2 * (units(c, s) - UB_SLOTS))
                nc.gpsimd.tensor_tensor(ub[:, s % UB_SLOTS, :, :], u[:, par, :, :],
                                        b_bc[:, s:s + 1, :].broadcast_to([P, DH, T]),
                                        ALU.mult).then_inc(s_ub, 1)

            def times_c(c, s, par, batch):
                i = POOL_STATES.index(s)
                wait(pool, s_c, 16 * len(POOL_RUNS) * (c + 1))
                wait(pool, s_scan, 2 * units(c, s))
                if par == 0:
                    wait(pool, s_carry, units(batch, s))
                nc.gpsimd.tensor_tensor(h[:, s % H_SLOTS, :, :], h[:, s % H_SLOTS, :, :],
                                        c_bc[:, i:i + 1, :].broadcast_to([P, DH, T]),
                                        ALU.mult).then_inc(s_hc_pool, 1)

            def norm_scalars(c):
                wait(pool, s_ln_in, 2 * c)
                nc.gpsimd.tensor_tensor(rstd[:, :, :], var_eps[:, :, :], neg_half[:, :, :],
                                        ALU.pow).then_inc(s_rstd, 1)
                wait(pool, s_rstd, c)
                nc.gpsimd.tensor_tensor(shift[:, :, :], neg_mean[:, :, :], rstd[:, :, :],
                                        ALU.mult).then_inc(s_ln, 1)

            def low_half(c, j):
                wait(pool, s_hid_hi, NH * c + (j + 1))
                nc.gpsimd.tensor_tensor(hid16[:, 1, j, :], hid[:, j % 2, :], hid16[:, 0, j, :],
                                        ALU.subtract).then_inc(s_hid_lo, 1)

            u_of(0, 0)
            for s in range(UB_AHEAD):
                times_b(0, s, 0)

            def step(c, par, batch, nxt, core, prev, last):
                for s in range(N):
                    ca, sa, pa = unit_at(c, s, UB_AHEAD, par)
                    for zone in range(2):
                        due = due_at(s, zone)
                        if (prev or last) and due("scalars"):
                            norm_scalars(c)
                        if nxt and due("u_of"):
                            u_of(c + 1, 1 - par)
                        for chunk, j in tiles("low_half", s, zone, c, prev, last):
                            low_half(chunk, j)
                        if zone == 0:
                            if core and (sa >= UB_AHEAD or nxt):
                                times_b(ca, sa, pa)
                        elif core and s - POOL_LAG in POOL_STATES:
                            times_c(c, s - POOL_LAG, par, batch)
            over_chunks(pool, step)

        @block.scalar
        def _(act):
            act.wait_ge(s_small_in, 16 * SMALL_LOADS)
            nc.scalar.activation(neg_a[:, :, :], a_raw[:, :, :], ACT.Exp).then_inc(s_a_exp, 1)
            act.wait_ge(s_wt_ps, 1)
            w_proj_t = p_y[:, 0, 0:DH * (R + BC)].rearrange("p (q r) -> p q r", q=DH)
            nc.scalar.copy(wt_proj[:, :, 0:R + BC], w_proj_t).then_inc(s_wt, 1)
            nc.scalar.copy(wt_proj[:, :, SECOND], w_proj_t[:, :, FIRST]).then_inc(s_wt, 1)
            nc.scalar.copy(wt_dt[0:R, :, :], p_y[0:R, 1, 0:DH * P].rearrange(
                "p (q r) -> p q r", q=DH)).then_inc(s_wt, 1)

            ffn_weights = ([wt_gate[:, q, :] for q in range(DH)] + [wt_up[:, q, :] for q in range(DH)]
                           + [wt_down[:, 3 * q:3 * q + 3, :].rearrange("p j d -> p (j d)") for q in range(2)])

            def weights_out(n):
                act.wait_ge(s_wt_ps, n + 2)
                nc.scalar.copy(ffn_weights[n], p_m_flat[:, 0:HID]).then_inc(s_wt, 1)

            def x_out(c, par):
                wait(act, s_xt_ps, c + 1)
                nc.scalar.copy(x_t[:, par, :, :], p_m[:, :, :]).then_inc(s_xt, 1)

            def rank_out(c):
                wait(act, s_proj_ps, c + 1)
                nc.scalar.copy(rank_t[0:R, :], p_m[0:R, 0, :]).then_inc(s_rank, 1)

            def bc_out(c, par):
                wait(act, s_proj_ps, c + 1)
                wait(act, s_rows_dram, 16 * c)
                nc.scalar.copy(bc_rows[FIRST, :], p_m[FIRST, 0, :]).then_inc(s_rows, 1)
                nc.scalar.copy(bc_parts[BOTH, par, :], p_m[BOTH, 0, :]).then_inc(s_part1, 1)

            def second_parts(c, par):
                wait(act, s_rest, c + 1)
                nc.scalar.copy(bc_mid[FIRST, :], bc_rest[FIRST, :]).then_inc(s_part2, 1)
                nc.scalar.copy(bc_parts[SECOND, par, :], bc_rest[SECOND, :]).then_inc(s_part2, 1)

            def softplus_in(c, par):
                wait(act, s_dt_ps, c + 1)
                nc.scalar.activation(sp_abs[:, :, :], p_m[:, :, :], ACT.Abs).then_inc(s_sp_abs, 1)
                nc.scalar.activation(dt[:, par, :, :], p_m[:, :, :], ACT.Relu).then_inc(s_sp_relu, 1)

            def softplus_exp(c):
                wait(act, s_sp_abs, c + 1)
                nc.scalar.activation(sp_abs[:, :, :], sp_abs[:, :, :], ACT.Exp, scale=-1.0).then_inc(s_sp_exp, 1)

            def softplus_log(c):
                wait(act, s_sp_exp, c + 1)
                nc.scalar.activation(sp_abs[:, :, :], sp_abs[:, :, :], ACT.Ln, bias=1.0).then_inc(s_sp_log, 1)

            def decay(c, s, par, q):
                wait(act, s_dt, c + 1)
                wait(act, s_scan, 2 * units(c, s) - 2 + q - 1)
                nc.scalar.activation(p_da[:, q, :], dt[:, par, q, :], ACT.Exp,
                                     scale=neg_a[:, q, s:s + 1]).then_inc(s_da, 1)

            def z_out(c):
                wait(act, s_y, N * (c + 1))
                nc.scalar.copy(z[:, :, :], p_y[:, :, :]).then_inc(s_z, 1)

            def norm1(c):
                wait(act, s_zt_ps, c + 1)
                wait(act, s_ln, c + 1)
                for k in range(TT):
                    nc.scalar.activation(x1[:, k, :], p_m_tok[:, k, :], ACT.Identity, bias=shift[:, 0, k:k + 1],
                                         scale=rstd[:, 0, k:k + 1]).then_inc(s_x1, 1)

            def x1_high(c):
                wait(act, s_x1t_ps, c + 1)
                nc.scalar.mul(x1_t[:, 0, :, :], p_m[:, :, :], X1_SCALE).then_inc(s_x1_hi, 1)

            def tanh_of(c, j):
                wait(act, s_gate_ps, NH * c + (j + 1))
                nc.scalar.activation(tanh_g[:, :], p_m[:, 0, :], ACT.Tanh,
                                     scale=0.5 / (QUANT * X1_SCALE)).then_inc(s_tanh, 1)

            def high_half(c, j):
                wait(act, s_hid, NH * c + (j + 1))
                nc.scalar.copy(hid16[:, 0, j, :], hid[:, j % 2, :]).then_inc(s_hid_hi, 1)

            def norm2(c):
                wait(act, s_ln, c + 2)
                wait(act, s_res, 2 * (c + 1))
                wait(act, s_out, 16 * (c + 1))
                for k in range(TT):
                    ins = nc.scalar.activation(res_n[:, k, :], res[:, k, :], ACT.Identity,
                                               bias=shift[:, 1, k:k + 1], scale=rstd[:, 1, k:k + 1])
                ins.then_inc(s_out_ready, 1)

            x_out(0, 0)
            rank_out(0)
            bc_out(0, 0)
            second_parts(0, 0)
            softplus_in(0, 0)
            softplus_exp(0)
            softplus_log(0)
            act.wait_ge(s_neg_a, 1)
            act.wait_ge(s_skip1, 1)
            for q in range(DH):
                decay(0, 0, 0, q)
            act.wait_ge(s_const, 1)
            for q in range(DH):
                nc.scalar.mul(skip_diag[:, q, :], ident[:, :], skip1[:, q:q + 1]).then_inc(s_skip_diag, 1)

            def step(c, par, batch, nxt, core, prev, last):
                for s in range(N):
                    ce, se, pe_ = unit_at(c, s, DA_AHEAD, par)
                    for zone in range(2):
                        due = due_at(s, zone)
                        if prev and due("z_out"):
                            z_out(c - 1)
                        if nxt and due("x_out"):
                            x_out(c + 1, 1 - par)
                        if nxt and due("rank_out"):
                            rank_out(c + 1)
                        if nxt and due("bc_out"):
                            bc_out(c + 1, 1 - par)
                        if nxt and due("second_parts"):
                            second_parts(c + 1, 1 - par)
                        if nxt and due("softplus_in"):
                            softplus_in(c + 1, 1 - par)
                        if nxt and due("softplus_exp"):
                            softplus_exp(c + 1)
                        if nxt and due("softplus_log"):
                            softplus_log(c + 1)
                        if prev and due("norm1"):
                            norm1(c - 1)
                        if prev and due("x1_high"):
                            x1_high(c - 1)
                        for chunk, j in tiles("high_half", s, zone, c, prev, last):
                            high_half(chunk, j)
                        for chunk, j in tiles("tanh", s, zone, c, prev, last):
                            tanh_of(chunk, j)
                        if last and due("norm2"):
                            norm2(c - 2)
                        if nxt and not prev and zone == 0 and s - AT["weights"][0] - 1 in range(WEIGHT_BATCHES):
                            weights_out(s - AT["weights"][0] - 1)
                        if core and (se >= DA_AHEAD or nxt):
                            decay(ce, se, pe_, zone)
            over_chunks(act, step)

        @block.vector
        def _(dve):
            nc.vector.memset(rank_t[R:R + 1, :], 1.0).then_inc(s_ones, 1)
            nc.vector.memset(mean_var[:, 1, :, :], 1.0).then_inc(s_ones, 1)
            nc.vector.memset(bc_parts[BC:R, :, :], 0.0).then_inc(s_ones, 1)
            dve.wait_ge(s_a_exp, 1)
            nc.vector.tensor_scalar_mul(neg_a[:, :, :], neg_a[:, :, :], -1.0).then_inc(s_neg_a, 1)
            nc.vector.tensor_scalar_add(skip1[:, :], skip_raw[:, :], 1.0).then_inc(s_skip1, 1)

            def weights_to_float():
                dve.wait_ge(s_w_in, 16 * len(w_rows))
                for rows in w_rows:
                    nc.vector.tensor_copy(rows, rows.bitcast(I32)).then_inc(s_wfloat, 1)

            def rest(c, par):
                wait(dve, s_rank, c + 1)
                wait(dve, s_part1, c + 1)
                nc.vector.tensor_tensor(bc_rest[BOTH, :], p_m[BOTH, 0, :], bc_parts[BOTH, par, :],
                                        ALU.subtract).then_inc(s_rest, 1)

            def third_part(c, par):
                wait(dve, s_part2, 2 * (c + 1))
                nc.vector.tensor_tensor(bc_parts[THIRD, par, :], bc_rest[FIRST, :], bc_mid[FIRST, :],
                                        ALU.subtract).then_inc(s_parts, 1)

            def dt_of(c, par):
                wait(dve, s_sp_relu, c + 1)
                wait(dve, s_sp_log, c + 1)
                nc.vector.tensor_tensor(dt[:, par, :, :], dt[:, par, :, :], sp_abs[:, :, :],
                                        ALU.add).then_inc(s_dt, 1)

            def scan(c, s, par, batch, q):
                wait(dve, s_da, 2 * units(c, s) - 1 + q)
                if q == 0:
                    wait(dve, s_ub, units(c, s))
                    ch, sh, _ = unit_at(c, s, -H_SLOTS, par)
                    if not (isinstance(ch, int) and ch < 0):
                        wait(dve, s_y, sums(ch, sh))
                if par == 0:
                    initial = 0.0
                else:
                    initial = h_carry[:, s, q:q + 1]
                    if q == 0:
                        wait(dve, s_carry, units(batch, s))
                nc.vector.tensor_tensor_scan(h[:, s % H_SLOTS, q, :], p_da[:, q, :], ub[:, s % UB_SLOTS, q, :],
                                             initial, ALU.mult, ALU.add).then_inc(s_scan, 1)

            def carry(c, s):
                wait(dve, s_scan, 2 * units(c, s))
                nc.vector.tensor_copy(h_carry[:, s, :], h[:, s % H_SLOTS, :, T - 1]).then_inc(s_carry, 1)

            def times_c(c, s, par, batch):
                i = DVE_STATES.index(s)
                wait(dve, s_c_ps, ND * c + (i + 1))
                wait(dve, s_scan, 2 * units(c, s))
                if par == 0:
                    wait(dve, s_carry, units(batch, s))
                nc.vector.tensor_tensor(h[:, s % H_SLOTS, :, :], h[:, s % H_SLOTS, :, :],
                                        p_c[:, :, :].broadcast_to([P, DH, T]),
                                        ALU.mult).then_inc(s_hc_dve, 1)

            def norm_stats(k, src):
                for t in range(TT):
                    nc.vector.bn_stats(stats[:, k, t, :], src[:, t, :]).then_inc(s_stats[k], 1)

            def norm_mean(k):
                for t in range(TT):
                    ins = nc.vector.bn_aggr(mean_var[:, k, t, :], stats[:, k, t, :])
                ins.then_inc(s_mean[k], 1)

            def norm_inputs(c, prev, last):
                if prev:
                    wait(dve, s_mean[0], c)
                if last:
                    wait(dve, s_mean[1], c - 1)
                nc.vector.tensor_scalar_add(var_eps[:, :, :], mean_var[:, :, :, 1], EPS).then_inc(s_ln_in, 1)
                nc.vector.tensor_scalar_mul(neg_mean[:, :, :], mean_var[:, :, :, 0], -1.0).then_inc(s_ln_in, 1)

            def x1_low(c):
                wait(dve, s_x1_hi, c + 1)
                nc.vector.scalar_tensor_tensor(x1_t[:, 1, :, :], p_m[:, :, :], X1_SCALE, x1_t[:, 0, :, :],
                                               ALU.mult, ALU.subtract).then_inc(s_x1_lo, 1)

            def silu_of(c, j):
                wait(dve, s_tanh, NH * c + (j + 1))
                nc.vector.scalar_tensor_tensor(silu_g[:, :], tanh_g[:, :], 1.0, p_m[:, 0, :],
                                               ALU.add, ALU.mult).then_inc(s_silu, 1)

            def hidden(c, j):
                wait(dve, s_up_ps, NH * c + (j + 1))
                wait(dve, s_silu, NH * c + (j + 1))
                if j >= 2:
                    wait(dve, s_hid_lo, NH * c + (j - 1))
                nc.vector.scalar_tensor_tensor(hid[:, j % 2, :], p_m[:, 1, :],
                                               H_SCALE / (2.0 * QUANT * QUANT * X1_SCALE * X1_SCALE),
                                               silu_g[:, :], ALU.mult, ALU.mult).then_inc(s_hid, 1)

            def residual(c, a):
                wait(dve, s_o_ps, TT * c + 2 * (a + 1))
                nc.vector.scalar_tensor_tensor(
                    res[:, 2 * a:2 * a + 2, :], p_o[:, :, :], 1.0 / (QUANT * H_SCALE),
                    x1[:, 2 * a:2 * a + 2, :], ALU.mult, ALU.add).then_inc(s_res, 1)

            rest(0, 0)
            third_part(0, 0)
            dt_of(0, 0)
            weights_to_float()

            def step(c, par, batch, nxt, core, prev, last):
                for s in range(N):
                    cb, sb_, pb = unit_at(c, s, -1, par)
                    last_unit = core and s > 0 or prev and s == 0
                    for zone in range(3):
                        due = due_at(s, zone)
                        if last:
                            for a in range(2):
                                if due(f"residual{a}"):
                                    residual(c - 2, a)
                        if nxt and due("rest"):
                            rest(c + 1, 1 - par)
                        if nxt and due("third_part"):
                            third_part(c + 1, 1 - par)
                        if prev and due("stats1"):
                            wait(dve, s_zt_ps, c)
                            norm_stats(0, p_m_tok)
                        if last and due("stats2"):
                            wait(dve, s_res, 2 * (c - 1))
                            norm_stats(1, res)
                        if nxt and due("dt_of"):
                            dt_of(c + 1, 1 - par)
                        if (prev or last) and due("norm_inputs"):
                            norm_inputs(c, prev, last)
                        if prev and due("x1_low"):
                            x1_low(c - 1)
                        if zone == 2:
                            if prev and s == AT["mean1"][0]:
                                norm_mean(0)
                            if last and s == AT["mean2"][0]:
                                norm_mean(1)
                        for chunk, j in tiles("silu", s, zone, c, prev, last):
                            silu_of(chunk, j)
                        for chunk, j in tiles("hidden", s, zone, c, prev, last):
                            hidden(chunk, j)
                        if zone == 0:
                            if core:
                                scan(c, s, par, batch, 0)
                            if last_unit and pb == 0:
                                carry(cb, sb_)
                        elif zone == 1:
                            if prev and s == AT["mean1"][0]:
                                wait(dve, s_stats[0], TT * c)
                            if last and s == AT["mean2"][0]:
                                wait(dve, s_stats[1], TT * (c - 1))
                            if core:
                                scan(c, s, par, batch, 1)
                        elif last_unit and sb_ not in POOL_STATES:
                            times_c(cb, sb_, pb, batch)
            over_chunks(dve, step)

        @block.tensor
        def _(pe):
            pe.wait_ge(s_const, 1)
            pe.wait_ge(s_small_in, 16 * SMALL_LOADS)
            for q in range(DH):
                nc.tensor.transpose(p_y[:, 0, q * (R + BC):(q + 1) * (R + BC)],
                                    w_xproj_rows[:, q * P:(q + 1) * P], ident[0:R + BC, 0:R + BC])
            for q in range(DH):
                ins = nc.tensor.transpose(p_y[0:R, 1, q * P:(q + 1) * P], w_dt_rows[:, q, :], ident[:, :])
            ins.then_inc(s_wt_ps, 1)

            def weights_transposed(n):
                if n == 0:
                    pe.wait_ge(s_wfloat, len(w_rows))
                    pe.wait_ge(s_sp_relu, 2)
                else:
                    pe.wait_ge(s_wt, 3 + n)
                for b in range(NH):
                    if n < 2 * DH:
                        rows = w_rows[n // DH].rearrange("p (j d) -> p j d", d=D)
                        block = rows[:, b, (n % DH) * P:(n % DH + 1) * P]
                    else:
                        j = 3 * (n - 2 * DH) + b // DH
                        block = w_rows[2 + b % DH][:, j * P:(j + 1) * P]
                    ins = nc.tensor.transpose(p_m_flat[:, b * P:(b + 1) * P], block, ident[:, :])
                ins.then_inc(s_wt_ps, 1)

            def x_transposed(c):
                wait(pe, s_x_in, 16 * (c + 1))
                if isinstance(c, int) and c < 2:
                    wait(pe, s_sp_relu, c)
                elif isinstance(c, int) and c == 2:
                    pe.wait_ge(s_wt, 3 + WEIGHT_BATCHES)
                else:
                    wait(pe, s_hid, NH * (c - 2))
                for q in range(DH):
                    for k in range(TT):
                        ins = nc.tensor.transpose(p_m[:, q, k * P:(k + 1) * P],
                                                  x_in[:, k, q * P:(q + 1) * P], ident[:, :])
                ins.then_inc(s_xt_ps, 1)

            def project(c, par):
                wait(pe, s_xt, c + 1)
                for q in range(DH):
                    ins = nc.tensor.matmul(p_m[:, 0, :], wt_proj[:, q, :], x_t[:, par, q, :],
                                           start=(q == 0), stop=(q == DH - 1))
                ins.then_inc(s_proj_ps, 1)

            def project_dt(c):
                wait(pe, s_rank, c + 1)
                wait(pe, s_rest, c + 1)
                for q in range(DH):
                    ins = nc.tensor.matmul(p_m[:, q, :], wt_dt[:, q, :], rank_t[:, :], start=True, stop=True)
                ins.then_inc(s_dt_ps, 1)

            def broadcast_c(c, s, par):
                i = DVE_STATES.index(s)
                wait(pe, s_parts, c + 1)
                wait(pe, s_hc_dve, ND * c + i)
                nc.tensor.matmul(p_c[:, 0, :], selector[:, s, :], bc_parts[:, par, :],
                                 start=True, stop=True).then_inc(s_c_ps, 1)

            def sum_states(c, s, par):
                if s == SUM_ORDER[0]:
                    wait(pe, s_z, c)
                    for q in range(DH):
                        nc.tensor.matmul(p_y[:, q, :], skip_diag[:, q, :], x_t[:, par, q, :],
                                         start=True, stop=False)
                wait_hc(pe, c, s)
                for q in range(DH):
                    ins = nc.tensor.matmul(p_y[:, q, :], ident[:, :], h[:, s % H_SLOTS, q, :],
                                           start=False, stop=(s == SUM_ORDER[-1]))
                ins.then_inc(s_y, 1)

            def z_transposed(c, nxt, last):
                wait(pe, s_z, c + 1)
                if nxt:
                    wait(pe, s_sp_relu, c + 3)
                elif last:
                    wait(pe, s_hid, NH * c)
                for k in range(TT):
                    for q in range(DH):
                        ins = nc.tensor.transpose(p_m_tok[:, k, q * P:(q + 1) * P],
                                                  z[:, q, k * P:(k + 1) * P], ident[:, :])
                ins.then_inc(s_zt_ps, 1)

            def x1_transposed(c):
                wait(pe, s_x1, TT * (c + 1))
                for q in range(DH):
                    for k in range(TT):
                        ins = nc.tensor.transpose(p_m[:, q, k * P:(k + 1) * P],
                                                  x1[:, k, q * P:(q + 1) * P], ident[:, :])
                ins.then_inc(s_x1t_ps, 1)

            def gate_up(c, j):
                wait(pe, s_x1_lo, c + 1)
                for a, w, free, done in ((0, wt_gate, s_silu, s_gate_ps), (1, wt_up, s_hid, s_up_ps)):
                    if j:
                        wait(pe, free, NH * c + j)
                    for n in range(2 * DH):
                        ins = nc.tensor.matmul(p_m[:, a, :], w[:, n % DH, j * P:(j + 1) * P],
                                               x1_t[:, n // DH, n % DH, :],
                                               start=(n == 0), stop=(n == 2 * DH - 1))
                    ins.then_inc(done, 1)

            def down(c, k):
                if k == 0:
                    wait(pe, s_hid_lo, NH * (c + 1))
                if k % 2 == 0:
                    wait(pe, s_res, 2 * c + k // 2)
                for n in range(2 * NH):
                    ins = nc.tensor.matmul(p_o[:, k % 2, :], hid16[:, n // NH, n % NH, k * P:(k + 1) * P],
                                           wt_down[:, n % NH, :], start=(n == 0), stop=(n == 2 * NH - 1))
                ins.then_inc(s_o_ps, 1)

            x_transposed(0)
            pe.wait_ge(s_wt, 3)
            project(0, 0)
            pe.wait_ge(s_ones, 3)
            project_dt(0)
            pe.wait_ge(s_const, 4)
            pe.wait_ge(s_skip_diag, 2)

            def step(c, par, batch, nxt, core, prev, last):
                for s in range(N):
                    for zone in range(3):
                        due = due_at(s, zone)
                        if last:
                            for k in range(TT):
                                if due(f"down{k}"):
                                    down(c - 2, k)
                        if nxt and due("x_transposed"):
                            x_transposed(c + 1)
                        if nxt and due("project"):
                            project(c + 1, 1 - par)
                        if nxt and due("project_dt"):
                            project_dt(c + 1)
                        if prev and due("z_transposed"):
                            z_transposed(c - 1, nxt, last)
                        if prev and due("x1_transposed"):
                            x1_transposed(c - 1)
                        if nxt and not prev and zone == 1 and s - AT["weights"][0] in range(WEIGHT_BATCHES):
                            weights_transposed(s - AT["weights"][0])
                        for chunk, j in tiles("gate_up", s, zone, c, prev, last):
                            gate_up(chunk, j)
                        if zone == 0:
                            cb, sb_, pb = unit_at(c, s, -C_LAG, par)
                            if (core if s >= C_LAG else prev) and sb_ in DVE_STATES:
                                broadcast_c(cb, sb_, pb)
                        else:
                            lag = sorted(SUM_LAG.values())[-zone]
                            cy, sy, py = unit_at(c, s, -lag, par)
                            if SUM_LAG[sy in POOL_STATES] == lag and (core and s >= lag or prev and s < lag):
                                sum_states(cy, sy, py)
            over_chunks(pe, step)


_INS = ['L0_attn_x', 'L0_attn_W_xproj', 'L0_attn_W_dt', 'L0_attn_b_dt', 'L0_attn_A_log', 'L0_attn_Dp',
        'L0_ffn_w_gate', 'L0_ffn_w_up', 'L0_ffn_w_down']


def kernel(**inputs):
    import numpy as _np
    import concourse.bacc as _bacc
    from concourse import mybir as _mybir
    from concourse.bass_utils import run_bass_kernel_spmd as _run

    nc = _bacc.Bacc("TRN2", target_bir_lowering=False, num_devices=1)
    arrays, args = {}, []
    for name in _INS:
        a = _np.ascontiguousarray(inputs[name])
        arrays[f"in_{name}"] = a
        args.append(nc.dram_tensor(f"in_{name}", a.shape, _mybir.dt.from_np(a.dtype), kind="ExternalInput").ap())
    out = nc.dram_tensor("out_x", inputs['L0_attn_x'].shape, _mybir.dt.float32, kind="ExternalOutput").ap()
    mamba_ffn_block(nc, *args, out)
    r = _run(nc, [arrays], core_ids=[0])
    return r.results[0]["out_x"]
```
